# Optimizing a Trainium2 kernel written in Bass

```python
import numpy as np
import jax
import jax.numpy as jnp

def _softmax(x, axis=-1):
    return jax.nn.softmax(x, axis=axis)

def _gelu(x):
    return jax.nn.gelu(x, approximate=True)

def _silu(x):
    return jax.nn.silu(x)

def _sigmoid(x):
    return jax.nn.sigmoid(x)

def _layernorm(x, axis=-1, eps=1e-05):
    m = jnp.mean(x, axis=axis, keepdims=True)
    v = jnp.var(x, axis=axis, keepdims=True)
    return (x - m) / jnp.sqrt(v + eps)

def _scatter_add(tgt, idx, src, axis=0):
    return tgt.at[idx].add(src)

def _segment_sum(src, seg, n):
    return jax.ops.segment_sum(src, seg, n)
kernel_name = 'mk_gnn_resnorm_d4_gnn_r32_52cdfe'

def setup_inputs(seed: int=0):
    np.random.seed(seed)
    _w = jnp.asarray

    def _rec_inputs():
        import jax
        import jax.numpy as jnp
        _gk = jax.random.key(seed)
        x = -0.000202 + 1 * jax.random.normal(jax.random.fold_in(_gk, 1), (3125, 128), jnp.float32)
        src = jax.random.randint(jax.random.fold_in(_gk, 2), (50000,), 0, 3125, jnp.int32)
        dst = jnp.minimum((3125 * jax.random.uniform(jax.random.fold_in(_gk, 3), (50000,)) ** 2.0).astype(jnp.int32), 99999)
        _o = jnp.argsort(dst, stable=True)
        src = src[_o]
        dst = dst[_o]
        edge_attr_32 = 0.000196303 + 1.00016 * jax.random.normal(jax.random.fold_in(_gk, 12), (50000, 32), jnp.float32)
        return (x, src, dst, edge_attr_32)
    x, src, dst, edge_attr_32 = _rec_inputs()

    def _L0_gnn_setup():
        import jax, jax.numpy as jnp
        import numpy as np
        N = 50000
        E = 18750
        F_IN = 128
        F_HID = 512

        def gcn_conv(x, edge_index, W, b):
            n = x.shape[0]
            loop = jnp.arange(n)
            src = jnp.concatenate([edge_index[0], loop])
            dst = jnp.concatenate([edge_index[1], loop])
            xw = x @ W.T
            deg = jax.ops.segment_sum(jnp.ones_like(dst, dtype=x.dtype), dst, num_segments=n)
            dinv = jnp.where(deg > 0, jax.lax.rsqrt(deg), 0.0)
            norm = dinv[src] * dinv[dst]
            msg = xw[src] * norm[:, None]
            out = jax.ops.segment_sum(msg, dst, num_segments=n)
            return out + b
        key = jax.random.key(seed)
        k = jax.random.split(key, 7)
        x = jax.random.normal(k[0], (N, F_IN), dtype=jnp.float32)
        edge_index = jax.random.randint(k[1], (2, E), 0, N, dtype=jnp.int64)
        s1 = float(np.sqrt(1.0 / F_IN))
        s2 = float(np.sqrt(1.0 / F_HID))
        W1 = jax.random.uniform(k[2], (F_HID, F_IN), jnp.float32, -s1, s1)
        b1 = jnp.zeros((F_HID,), jnp.float32)
        W2 = jax.random.uniform(k[3], (F_IN, F_HID), jnp.float32, -s2, s2)
        b2 = jnp.zeros((F_IN,), jnp.float32)
        return {'x': x, 'edge_index': edge_index, 'W1': W1, 'b1': b1, 'W2': W2, 'b2': b2}
    _L0_gnn_all = _L0_gnn_setup()
    _L0_gnn_in = {k: v for k, v in _L0_gnn_all.items() if k in ('W1', 'b1', 'W2', 'b2')}
    del _L0_gnn_all

    def _L1_gnn_setup():
        import jax, jax.numpy as jnp
        import numpy as np
        N_NODES = 50000
        N_EDGES = 25000
        D = 128
        EDGE_DIM = 32
        BN_EPS = 1e-05

        def _batchnorm(x, gamma, beta):
            mean = jnp.mean(x, axis=0)
            var = jnp.var(x, axis=0)
            return (x - mean) * jax.lax.rsqrt(var + BN_EPS) * gamma + beta
        key = jax.random.key(seed)
        ks = jax.random.split(key, 8)
        s_e = 1.0 / np.sqrt(EDGE_DIM)
        s_d = 1.0 / np.sqrt(D)
        return {'x': jax.random.normal(ks[0], (N_NODES, D), dtype=jnp.float32), 'edge_index': jax.random.randint(ks[1], (2, N_EDGES), 0, N_NODES, dtype=jnp.int32), 'edge_attr': jax.random.normal(ks[2], (N_EDGES, EDGE_DIM), dtype=jnp.float32), 'epsilon': jnp.zeros((1,), dtype=jnp.float32), 'We': jax.random.uniform(ks[3], (EDGE_DIM, D), jnp.float32, -s_e, s_e), 'be': jnp.zeros((D,), jnp.float32), 'W1': jax.random.uniform(ks[4], (D, D), jnp.float32, -s_d, s_d), 'b1': jnp.zeros((D,), jnp.float32), 'g1': jnp.ones((D,), jnp.float32), 'beta1': jnp.zeros((D,), jnp.float32), 'W2': jax.random.uniform(ks[5], (D, D), jnp.float32, -s_d, s_d), 'b2': jnp.zeros((D,), jnp.float32), 'g2': jnp.ones((D,), jnp.float32), 'beta2': jnp.zeros((D,), jnp.float32)}
    _L1_gnn_all = _L1_gnn_setup()
    _L1_gnn_in = {k: v for k, v in _L1_gnn_all.items() if k in ('epsilon', 'We', 'be', 'W1', 'b1', 'g1', 'beta1', 'W2', 'b2', 'g2', 'beta2')}
    del _L1_gnn_all

    def _L2_gnn_setup():
        import jax, jax.numpy as jnp
        import numpy as np
        NEG_SLOPE = 0.01
        N_NODES = 50000
        N_EDGES = 18750
        D = 128

        def _sage_gcn_layer(h, src, dst, W, b, n_nodes):
            msg = jax.ops.segment_sum(h[src], dst, num_segments=n_nodes)
            deg = jax.ops.segment_sum(jnp.ones((src.shape[0],), h.dtype), dst, num_segments=n_nodes)
            h_neigh = (msg + h) / (deg[:, None] + 1.0)
            return h_neigh @ W + b
        key = jax.random.key(seed)
        k = jax.random.split(key, 6)
        x = jax.random.normal(k[0], (N_NODES, D), dtype=jnp.float32)
        src_idx = jax.random.randint(k[1], (N_EDGES,), 0, N_NODES, dtype=jnp.int64 if jax.config.jax_enable_x64 else jnp.int32).astype(jnp.int32)
        dst_idx = jax.random.randint(k[2], (N_EDGES,), 0, N_NODES, dtype=jnp.int32)
        W1 = jax.random.normal(k[3], (D, D), dtype=jnp.float32) * (1.0 / np.sqrt(D))
        b1 = jnp.zeros((D,), dtype=jnp.float32)
        W2 = jax.random.normal(k[4], (D, D), dtype=jnp.float32) * (1.0 / np.sqrt(D))
        b2 = jnp.zeros((D,), dtype=jnp.float32)
        return {'x': x, 'src_idx': src_idx, 'dst_idx': dst_idx, 'W1': W1, 'b1': b1, 'W2': W2, 'b2': b2}
    _L2_gnn_all = _L2_gnn_setup()
    _L2_gnn_in = {k: v for k, v in _L2_gnn_all.items() if k in ('W1', 'b1', 'W2', 'b2')}
    del _L2_gnn_all

    def _L3_gnn_setup():
        import jax, jax.numpy as jnp
        import numpy as np
        N_NODES = 50000
        N_EDGES = 12500
        D = 128
        NUM_LAYERS = 3
        DELTA = 4.0
        BN_EPS = 1e-05
        LN_EPS = 1e-05
        STD_EPS = 1e-30
        N_AGG = 4
        N_SCAL = 3

        def _pna_layer(h, src, dst, Mw, Mb, Uw, Ub, bn_g, bn_b, mix_w, mix_b):
            N = h.shape[0]
            msg = jnp.concatenate([h[src], h[dst]], axis=-1) @ Mw.T + Mb
            deg = jax.ops.segment_sum(jnp.ones((msg.shape[0],), msg.dtype), dst, num_segments=N)
            s1 = jax.ops.segment_sum(msg, dst, num_segments=N)
            s2 = jax.ops.segment_sum(msg * msg, dst, num_segments=N)
            mx = jax.ops.segment_max(msg, dst, num_segments=N)
            mn = jax.ops.segment_min(msg, dst, num_segments=N)
            degc = deg[:, None]
            mean = s1 / degc
            var = jax.nn.relu(s2 / degc - mean * mean)
            std = jnp.sqrt(var + STD_EPS)
            agg = jnp.concatenate([mx, mn, std, var], axis=-1)
            logd = jnp.log(deg + 1.0)[:, None]
            h_neigh = jnp.concatenate([agg, agg * (logd / DELTA), agg * (DELTA / logd)], axis=-1)
            u = jnp.concatenate([h, h_neigh], axis=-1) @ Uw.T + Ub
            u = u * jnp.sqrt(1.0 / N)
            mu = jnp.mean(u, axis=0)
            v = jnp.mean((u - mu) ** 2, axis=0)
            u = (u - mu) / jnp.sqrt(v + BN_EPS) * bn_g + bn_b
            out = jax.nn.leaky_relu(u @ mix_w.T + mix_b, 0.01)
            return out + h
        key = jax.random.key(seed)
        ks = jax.random.split(key, 8)
        L = NUM_LAYERS
        s = 0.05
        feat = jax.random.normal(ks[0], (N_NODES, D), jnp.float32)
        src = jax.random.randint(ks[1], (N_EDGES,), 0, N_NODES, dtype=jnp.int32)
        dst = jax.random.randint(ks[2], (N_EDGES,), 0, N_NODES, dtype=jnp.int32)
        u_in = (N_AGG * N_SCAL + 1) * D
        Mw = jax.random.normal(ks[3], (L, D, 2 * D), jnp.float32) * s
        Mb = jnp.zeros((L, D), jnp.float32)
        Uw = jax.random.normal(ks[4], (L, D, u_in), jnp.float32) * s
        Ub = jnp.zeros((L, D), jnp.float32)
        bn_g = jnp.ones((L, D), jnp.float32)
        bn_b = jnp.zeros((L, D), jnp.float32)
        mix_w = jax.random.normal(ks[5], (L, D, D), jnp.float32) * s
        mix_b = jnp.zeros((L, D), jnp.float32)
        ln_g = jnp.ones((L, D), jnp.float32)
        ln_b = jnp.zeros((L, D), jnp.float32)
        return dict(feat=feat, src=src, dst=dst, Mw=Mw, Mb=Mb, Uw=Uw, Ub=Ub, bn_g=bn_g, bn_b=bn_b, mix_w=mix_w, mix_b=mix_b, ln_g=ln_g, ln_b=ln_b)
    _L3_gnn_all = _L3_gnn_setup()
    _L3_gnn_in = {k: v for k, v in _L3_gnn_all.items() if k in ('Mw', 'Mb', 'Uw', 'Ub', 'bn_g', 'bn_b', 'mix_w', 'mix_b', 'ln_g', 'ln_b')}
    del _L3_gnn_all
    return {'x': x, 'src': src, 'dst': dst, 'edge_attr_32': edge_attr_32, 'L0_gnn_W1': _L0_gnn_in['W1'], 'L0_gnn_b1': _L0_gnn_in['b1'], 'L0_gnn_W2': _L0_gnn_in['W2'], 'L0_gnn_b2': _L0_gnn_in['b2'], 'L1_gnn_epsilon': _L1_gnn_in['epsilon'], 'L1_gnn_We': _L1_gnn_in['We'], 'L1_gnn_be': _L1_gnn_in['be'], 'L1_gnn_W1': _L1_gnn_in['W1'], 'L1_gnn_b1': _L1_gnn_in['b1'], 'L1_gnn_g1': _L1_gnn_in['g1'], 'L1_gnn_beta1': _L1_gnn_in['beta1'], 'L1_gnn_W2': _L1_gnn_in['W2'], 'L1_gnn_b2': _L1_gnn_in['b2'], 'L1_gnn_g2': _L1_gnn_in['g2'], 'L1_gnn_beta2': _L1_gnn_in['beta2'], 'L2_gnn_W1': _L2_gnn_in['W1'], 'L2_gnn_b1': _L2_gnn_in['b1'], 'L2_gnn_W2': _L2_gnn_in['W2'], 'L2_gnn_b2': _L2_gnn_in['b2'], 'L3_gnn_Mw': _L3_gnn_in['Mw'], 'L3_gnn_Mb': _L3_gnn_in['Mb'], 'L3_gnn_Uw': _L3_gnn_in['Uw'], 'L3_gnn_Ub': _L3_gnn_in['Ub'], 'L3_gnn_bn_g': _L3_gnn_in['bn_g'], 'L3_gnn_bn_b': _L3_gnn_in['bn_b'], 'L3_gnn_mix_w': _L3_gnn_in['mix_w'], 'L3_gnn_mix_b': _L3_gnn_in['mix_b'], 'L3_gnn_ln_g': _L3_gnn_in['ln_g'], 'L3_gnn_ln_b': _L3_gnn_in['ln_b']}

def reference(x, src, dst, edge_attr_32, L0_gnn_W1, L0_gnn_b1, L0_gnn_W2, L0_gnn_b2, L1_gnn_epsilon, L1_gnn_We, L1_gnn_be, L1_gnn_W1, L1_gnn_b1, L1_gnn_g1, L1_gnn_beta1, L1_gnn_W2, L1_gnn_b2, L1_gnn_g2, L1_gnn_beta2, L2_gnn_W1, L2_gnn_b1, L2_gnn_W2, L2_gnn_b2, L3_gnn_Mw, L3_gnn_Mb, L3_gnn_Uw, L3_gnn_Ub, L3_gnn_bn_g, L3_gnn_bn_b, L3_gnn_mix_w, L3_gnn_mix_b, L3_gnn_ln_g, L3_gnn_ln_b):
    import jax
    import jax.numpy as jnp

    def _L0_gnn_ref(x, edge_index, W1, b1, W2, b2):
        import jax, jax.numpy as jnp
        import numpy as np
        N = 50000
        E = 18750
        F_IN = 128
        F_HID = 512

        def gcn_conv(x, edge_index, W, b):
            n = x.shape[0]
            loop = jnp.arange(n)
            src = jnp.concatenate([edge_index[0], loop])
            dst = jnp.concatenate([edge_index[1], loop])
            xw = x @ W.T
            deg = jax.ops.segment_sum(jnp.ones_like(dst, dtype=x.dtype), dst, num_segments=n)
            dinv = jnp.where(deg > 0, jax.lax.rsqrt(deg), 0.0)
            norm = dinv[src] * dinv[dst]
            msg = xw[src] * norm[:, None]
            out = jax.ops.segment_sum(msg, dst, num_segments=n)
            return out + b
        h = gcn_conv(x.astype(jnp.float32), edge_index, W1, b1)
        h = jax.nn.relu(h)
        h = gcn_conv(h, edge_index, W2, b2)
        return jax.nn.relu(h)

    def _L1_gnn_ref(x, edge_index, edge_attr, epsilon, We, be, W1, b1, g1, beta1, W2, b2, g2, beta2):
        import jax, jax.numpy as jnp
        import numpy as np
        N_NODES = 50000
        N_EDGES = 25000
        D = 128
        EDGE_DIM = 32
        BN_EPS = 1e-05

        def _batchnorm(x, gamma, beta):
            mean = jnp.mean(x, axis=0)
            var = jnp.var(x, axis=0)
            return (x - mean) * jax.lax.rsqrt(var + BN_EPS) * gamma + beta
        src, dst = (edge_index[0], edge_index[1])
        edge_feat = jax.nn.relu(edge_attr @ We + be)
        messages = x[src] + edge_feat
        agg = jax.ops.segment_sum(messages, dst, num_segments=x.shape[0])
        h = (1.0 + epsilon) * x + agg
        h = jax.nn.relu(_batchnorm(h @ W1 + b1, g1, beta1))
        h = jax.nn.relu(_batchnorm(h @ W2 + b2, g2, beta2))
        return h

    def _L2_gnn_ref(x, src_idx, dst_idx, W1, b1, W2, b2):
        import jax, jax.numpy as jnp
        import numpy as np
        NEG_SLOPE = 0.01
        N_NODES = 50000
        N_EDGES = 18750
        D = 128

        def _sage_gcn_layer(h, src, dst, W, b, n_nodes):
            msg = jax.ops.segment_sum(h[src], dst, num_segments=n_nodes)
            deg = jax.ops.segment_sum(jnp.ones((src.shape[0],), h.dtype), dst, num_segments=n_nodes)
            h_neigh = (msg + h) / (deg[:, None] + 1.0)
            return h_neigh @ W + b
        n = x.shape[0]
        h = _sage_gcn_layer(x, src_idx, dst_idx, W1, b1, n)
        h = jnp.where(h >= 0, h, NEG_SLOPE * h)
        out = _sage_gcn_layer(h, src_idx, dst_idx, W2, b2, n)
        return out

    def _L3_gnn_ref(feat, src, dst, Mw, Mb, Uw, Ub, bn_g, bn_b, mix_w, mix_b, ln_g, ln_b):
        import jax, jax.numpy as jnp
        import numpy as np
        N_NODES = 50000
        N_EDGES = 12500
        D = 128
        NUM_LAYERS = 3
        DELTA = 4.0
        BN_EPS = 1e-05
        LN_EPS = 1e-05
        STD_EPS = 1e-30
        N_AGG = 4
        N_SCAL = 3

        def _pna_layer(h, src, dst, Mw, Mb, Uw, Ub, bn_g, bn_b, mix_w, mix_b):
            N = h.shape[0]
            msg = jnp.concatenate([h[src], h[dst]], axis=-1) @ Mw.T + Mb
            deg = jax.ops.segment_sum(jnp.ones((msg.shape[0],), msg.dtype), dst, num_segments=N)
            s1 = jax.ops.segment_sum(msg, dst, num_segments=N)
            s2 = jax.ops.segment_sum(msg * msg, dst, num_segments=N)
            mx = jax.ops.segment_max(msg, dst, num_segments=N)
            mn = jax.ops.segment_min(msg, dst, num_segments=N)
            degc = deg[:, None]
            mean = s1 / degc
            var = jax.nn.relu(s2 / degc - mean * mean)
            std = jnp.sqrt(var + STD_EPS)
            agg = jnp.concatenate([mx, mn, std, var], axis=-1)
            logd = jnp.log(deg + 1.0)[:, None]
            h_neigh = jnp.concatenate([agg, agg * (logd / DELTA), agg * (DELTA / logd)], axis=-1)
            u = jnp.concatenate([h, h_neigh], axis=-1) @ Uw.T + Ub
            u = u * jnp.sqrt(1.0 / N)
            mu = jnp.mean(u, axis=0)
            v = jnp.mean((u - mu) ** 2, axis=0)
            u = (u - mu) / jnp.sqrt(v + BN_EPS) * bn_g + bn_b
            out = jax.nn.leaky_relu(u @ mix_w.T + mix_b, 0.01)
            return out + h
        N = feat.shape[0]
        loops = jnp.arange(N, dtype=src.dtype)
        src_sl = jnp.concatenate([src, loops])
        dst_sl = jnp.concatenate([dst, loops])
        h = feat
        for l in range(NUM_LAYERS):
            h = _pna_layer(h, src_sl, dst_sl, Mw[l], Mb[l], Uw[l], Ub[l], bn_g[l], bn_b[l], mix_w[l], mix_b[l])
            mu = jnp.mean(h, axis=-1, keepdims=True)
            v = jnp.mean((h - mu) ** 2, axis=-1, keepdims=True)
            h = (h - mu) / jnp.sqrt(v + LN_EPS) * ln_g[l] + ln_b[l]
            h = jax.nn.elu(h)
        return h
    edge_index = jnp.stack([src, dst])
    x = _layernorm(x + _L0_gnn_ref(x, edge_index, L0_gnn_W1, L0_gnn_b1, L0_gnn_W2, L0_gnn_b2), axis=-1)
    x = _layernorm(x + _L1_gnn_ref(x, edge_index, edge_attr_32, L1_gnn_epsilon, L1_gnn_We, L1_gnn_be, L1_gnn_W1, L1_gnn_b1, L1_gnn_g1, L1_gnn_beta1, L1_gnn_W2, L1_gnn_b2, L1_gnn_g2, L1_gnn_beta2), axis=-1)
    x = _layernorm(x + _L2_gnn_ref(x, src, dst, L2_gnn_W1, L2_gnn_b1, L2_gnn_W2, L2_gnn_b2), axis=-1)
    x = _layernorm(x + _L3_gnn_ref(x, src, dst, L3_gnn_Mw, L3_gnn_Mb, L3_gnn_Uw, L3_gnn_Ub, L3_gnn_bn_g, L3_gnn_bn_b, L3_gnn_mix_w, L3_gnn_mix_b, L3_gnn_ln_g, L3_gnn_ln_b), axis=-1)
    return x

_drawn_inputs = setup_inputs


def setup_inputs(seed=0):
    import zlib

    import numpy as np

    out = dict(_drawn_inputs(seed))
    spreads = {'L0_gnn_b1': (0.0, 0.1),
     'L0_gnn_b2': (0.0, 0.1),
     'L1_gnn_be': (0.0, 0.1),
     'L1_gnn_b1': (0.0, 0.8),
     'L1_gnn_g1': (1.0, 0.2),
     'L1_gnn_beta1': (0.0, 0.1),
     'L1_gnn_b2': (0.0, 0.8),
     'L1_gnn_g2': (1.0, 0.2),
     'L1_gnn_beta2': (0.0, 0.1),
     'L2_gnn_b1': (0.0, 0.1),
     'L2_gnn_b2': (0.0, 0.1),
     'L3_gnn_Mb': (0.0, 0.8),
     'L3_gnn_Ub': (0.0, 0.8),
     'L3_gnn_bn_g': (1.0, 0.2),
     'L3_gnn_bn_b': (0.0, 0.1),
     'L3_gnn_mix_b': (0.0, 0.1),
     'L3_gnn_ln_g': (1.0, 0.2),
     'L3_gnn_ln_b': (0.0, 0.1)}
    factors = {'L0_gnn_W1': 3.26}
    for name, (base, spread) in spreads.items():
        noise = np.random.default_rng([zlib.crc32(name.encode()), seed]).standard_normal(out[name].shape)
        drawn = base * np.exp(spread * noise) if base else spread * noise
        out[name] = jnp.asarray(drawn.astype(out[name].dtype))
    for name, factor in factors.items():
        out[name] = (out[name] * factor).astype(out[name].dtype)
    return out
```

```python
from contextlib import ExitStack

import numpy as np

import concourse.bass as bass
from concourse import mybir

F32 = mybir.dt.float32
BF16 = mybir.dt.bfloat16
F16 = mybir.dt.float16
I32 = mybir.dt.int32
ALU = mybir.AluOpType
ACT = mybir.ActivationFunctionType
AX = mybir.AxisListType
RMAX = bass.bass_isa.ReduceOp.max
ds = bass.ds

P = 128
N = 3125
E = 50000
D = 128
NB = -(-N // P)
NP = NB * P
HID = 512
HC = HID // P
AE = 33
LAYERS = 3
GB = 5
NG = NB // GB
QT = 4
CH = QT * P
NCH = 100
TG = NCH * QT
TD = -(-E // P) + 1
TD += TD % 2
EQ = -(-E // CH)
TP = TG
MID = NP // 2
BIG = 4096.0
FAR = -3.0e38
MARK = 1.5e38
ROUND = 8388608.0
BN_EPS = 1e-5
ACC = NB * P
V_X3, V_LAYER = 18, 6
S_X3, S_LAYER = 6, 3
MM3 = 5 * NB + 7
DVE_LAYER = 82
SLABS = [9, 8, 8]


WEIGHTS = {
    "L0_W1T": [P, HID], "L0_b1": [P, HC], "L0_W2T": [P, HC, D],
    "L1_W1": [P, D], "L1_W2": [P, D], "L1_cols": [P, 7],
    "L2_W1": [P, D], "L2_W2": [P, D],
    "rows": [P, 3, D],
    "M": [P, 3 * D], "U": [P, 4, 3 * D], "mix": [P, D],
    "L3_rows": [P, 5, D],
    "L3_cols": [P, 2],
}
LATER = ["U", "mix", "L3_rows", "L3_cols"]
ONCE = [w for w in WEIGHTS if w not in ("M", "U", "mix", "L3_rows", "L3_cols")]


def gnn_kernel(nc, ins, out):
    at_part = [nc.dram_tensor(f"at_part{i}", [NB, P, NB * P], BF16, kind="Internal").ap() for i in range(2)]
    a_dram = nc.dram_tensor("a_dram", [NP, D], F32, kind="Internal").ap()
    x3_dram = nc.dram_tensor("x3_dram", [P, NB, D], F32, kind="Internal").ap()
    scan_dram = nc.dram_tensor("scan_dram", [NCH * CH + 1, 2 * D], F32, kind="Internal").ap()
    mask_dram = nc.dram_tensor("mask_dram", [NCH, 2 * CH], BF16, kind="Internal").ap()

    with ExitStack() as ctx:
        def sb(name, shape, dt):
            return ctx.enter_context(nc.sbuf_tensor(name, shape, dt))

        def sem(name):
            return ctx.enter_context(nc.semaphore(name))

        psum = ctx.enter_context(nc.psum_tensor("psum", [P, 8 * 512], F32))

        identity = sb("identity", [P, P], F32)
        src_col = sb("src_col", [P, TP], I32)
        ranges = sb("ranges", [P, 64], I32)
        deg = sb("deg", [P, NB], F32)
        edge_sum = sb("edge_sum", [P, NB, D], F32)
        overflow = sb("overflow", [P, 1], I32)
        x = sb("x", [P, NB, D], F32)
        weights = {name: sb("w_" + name, shape, F32) for name, shape in WEIGHTS.items()}
        d_self = sb("d_self", [P, NB], F32)
        root = sb("root", [P, NB], F32)
        dinv = sb("dinv", [P, NB], F32)
        rdeg = sb("rdeg", [P, NB], F32)
        log4 = sb("log4", [P, NB], F32)
        inv4 = sb("inv4", [P, NB], F32)
        upto = sb("upto", [P, P], F32)
        ones = sb("ones", [P, P], F32)
        end_idx = sb("end_idx", [P, NB], I32)
        end_f = sb("end_f", [P, NB], F32)
        total_f = sb("total_f", [P, NB + 1], F32)
        some = sb("some", [P, NB], F32)
        far_row = sb("far_row", [1, 2 * D], F32)
        stats = sb("stats", [P, NB, 6], F32)
        mv = sb("mv", [P, NB, 2], F32)
        rstd = sb("rstd", [P, NB], F32)
        std = sb("std", [P, NB], F32)
        cstats = sb("cstats", [P, 7, 6], F32)
        cmv = sb("cmv", [P, 2], F32)
        cstd = sb("cstd", [P, 1], F32)
        cscale = sb("cscale", [P, 1], F32)
        cshift = sb("cshift", [P, 1], F32)
        eps = sb("eps", [P, 2], F32)
        one_eps = sb("one_eps", [P, 1], F32)

        bctx = ExitStack()

        def sbb(name, shape, dt):
            return bctx.enter_context(nc.sbuf_tensor(name, shape, dt))

        iota_src = sbb("iota_src", [P, NP], F16)
        iota_dst = sbb("iota_dst", [P, P], F32)
        block_base = sbb("block_base", [P, NB + 1], F32)
        zeros = sbb("zeros", [P, 512], BF16)
        ones_col = sbb("ones_col", [P, 1], F32)
        dst_col = sbb("dst_col", [P, TP], I32)
        src_off = sbb("src_off", [P, TP], F32)
        dst_f = sbb("dst_f", [P, TP], F32)
        onehot_src = sbb("onehot_src", [P, 2, NP], BF16)
        onehot_dst = sbb("onehot_dst", [P, 4, 2, P], BF16)
        deg_to = sbb("deg_to", [P, NB + 1], F32)
        onehot_sum = sbb("onehot_sum", [P, P], F32)
        attr_ring = sbb("attr_ring", [AE, 4, 2 * P], F32)
        attr_now = sbb("attr_now", [AE, 2 * P], F32)
        we = sbb("we", [AE, D], F32)
        ef32 = sbb("ef32", [P, 2, D], F32)
        ef_rest = sbb("ef_rest", [P, 2, D], F32)
        ef_split = sbb("ef_split", [P, 2, 2, 3 * D], BF16)
        a32 = sbb("a32", [P, NB * P], F32)
        a_part = [sbb(f"a_part{i}", [P, NB * P], BF16) for i in range(2)]
        a_most = sbb("a_most", [P, NB * P], BF16)
        most = sbb("most", [P, 2], F32)
        rows_i = sbb("rows_i", [P, CH], I32)
        prev_i = sbb("prev_i", [P, CH], I32)
        mask_rows = sbb("mask_rows", [P, 2, CH], BF16)
        rows_f = sbb("rows_f", [P, CH], F32)
        prev_f = sbb("prev_f", [P, CH], F32)
        t_min = sbb("t_min", [P, QT], F32)
        t_max = sbb("t_max", [P, QT], F32)
        t_next = sbb("t_next", [P, QT], F32)
        t_left = sbb("t_left", [P, QT], F32)
        b_lo = sbb("b_lo", [P, NB], F32)
        b_hi = sbb("b_hi", [P, NB], F32)
        touch = sbb("touch", [P, 2, NB], F32)
        reach = sbb("reach", [P, 2, NB], F32)
        reach_all = sbb("reach_all", [P, 2, NB], F32)
        rng_f = sbb("rng_f", [P, 64], F32)
        first = sbb("first", [P, NB + 1], F32)
        end = sbb("end", [P, NB + 1], F32)
        steps = sbb("steps", [P, NB], F32)

        bctx.close()

        hs = sb("hs", [P, NB, 6, D], BF16)
        slab = [sb(f"slab{i}", [P, NB * P], BF16) for i in range(3)]
        slab_rest = sb("slab_rest", [P, NB * P], BF16)
        agg = sb("agg", [P, NB, D], F32)
        g = sb("g", [P, NB, D], F32)
        ft = sb("ft", [P, NP], F32)
        ft2 = sb("ft2", [P, NP], F32)
        turned = sb("turned", [P, 2, 4 * D], F32)
        hidden = sb("hidden", [P, 2, HC, P], F32)
        idx_now = sb("idx_now", [P, QT, QT], I32)
        rows_g = sb("rows_g", [P, QT, QT, D], F32)
        marks = [sb(f"marks{i}", [P, 2 * CH], BF16) for i in range(2)]
        runs = [sb(f"runs{i}", [P, 2, CH], F32) for i in range(2)]
        run_rows = [sb(f"run_rows{i}", [P, QT, 2 * D], F32) for i in range(2)]
        var_tmp = sb("var_tmp", [P, 4, D], F32)
        u_row = sb("u_row", [P, 2, D], F32)
        ends = hs[:].rearrange("p b s f -> p (b s f)").bitcast(F32)[:, 0:NB * 2 * D].rearrange(
            "p (b s f) -> p b s f", b=NB, s=2)

        s_lists = sem("s_lists")
        s_we = sem("s_we")
        s_const = sem("s_const")
        s_prime = sem("s_prime")
        s_dve = sem("s_dve")
        s_casts = sem("s_casts")
        s_reach = sem("s_reach")
        s_reached = sem("s_reached")
        s_ranges = sem("s_ranges")
        s_mask = sem("s_mask")
        s_mask_out = sem("s_mask_out")
        s_attr = sem("s_attr")
        s_attr_now = sem("s_attr_now")
        s_ef_mm = sem("s_ef_mm")
        s_ef32 = sem("s_ef32")
        s_ef_hi = sem("s_ef_hi")
        s_ef_r1 = sem("s_ef_r1")
        s_ef_mid = sem("s_ef_mid")
        s_ef_lo = sem("s_ef_lo")
        s_oh = sem("s_oh")
        s_oh_sum = sem("s_oh_sum")
        s_tile = sem("s_tile")
        s_block = sem("s_block")
        s_deg_mm = sem("s_deg_mm")
        s_ev_first = sem("s_ev_first")
        s_ev_act = sem("s_ev_act")
        s_ev_dve = sem("s_ev_dve")
        s_part0 = sem("s_part0")
        s_part1 = sem("s_part1")
        s_most = sem("s_most")
        s_store0 = sem("s_store0")
        s_store1 = sem("s_store1")
        s_flag = sem("s_flag")

        s_w = sem("s_w")
        s_far = sem("s_far")
        s_node = sem("s_node")
        s_act = sem("s_act")
        s_rank = sem("s_rank")
        s_hi = sem("s_hi")
        s_r1 = sem("s_r1")
        s_mid = sem("s_mid")
        s_hs = sem("s_hs")
        s_slab = [sem(f"s_slab{i}") for i in range(3)]
        s_slab_rest = sem("s_slab_rest")
        s_rest_used = sem("s_rest_used")
        s_spmm = sem("s_spmm")
        s_agg = sem("s_agg")
        s_tr = sem("s_tr")
        s_trc = sem("s_trc")
        s_mm = sem("s_mm")
        s_res = sem("s_res")
        s_hid = sem("s_hid")
        s_hidr = sem("s_hidr")
        s_rows = sem("s_rows")
        s_bn = sem("s_bn")
        s_std = sem("s_std")
        s_x3 = sem("s_x3")
        s_lm = sem("s_lm")
        s_lw = sem("s_lw")
        s_merged = sem("s_merged")
        s_y = sem("s_y")
        s_neg = sem("s_neg")
        s_e = sem("s_e")
        s_grp = sem("s_grp")
        s_ab = sem("s_ab")
        s_a_out = sem("s_a_out")
        s_idx = sem("s_idx")
        s_gat = [sem(f"s_gat{i}") for i in range(QT)]
        s_mk = [sem(f"s_mk{i}") for i in range(2)]
        s_fwd = sem("s_fwd")
        s_scan = sem("s_scan")
        s_back = sem("s_back")
        s_rr = sem("s_rr")
        s_st = [sem(f"s_st{i}") for i in range(2)]
        s_var = sem("s_var")
        s_ends = [sem(f"s_ends{i}") for i in range(NG)]
        s_u = sem("s_u")
        s_ut = sem("s_ut")
        s_z = sem("s_z")
        s_out = sem("s_out")
        s_past = sem("s_past")

        lists = {"in_src_col": src_col, "in_dst_col": dst_col}
        N_CONST = 10
        block = ctx.enter_context(nc.Block())

        def bank(i):
            return psum[:, i * 512:(i + 1) * 512]

        def in_turn(eng, n, body):
            with eng.Fori(0, NB // n) as i:
                for s in range(n):
                    body(n * i + s, s, i)
            for s in range(NB % n):
                body(NB // n * n + s, s, NB // n)

        def load_pairs(eng, b):
            lo = eng.value_load(ranges[0:1, ds(b, 1)], min_val=0, max_val=NB * TD)
            hi = eng.value_load(ranges[0:1, ds(b + 1, 1)], min_val=1, max_val=NB * TD)
            off = eng.value_load(ranges[0:1, ds(b + 32, 1)], min_val=0, max_val=2 * NB * TD)
            return lo, hi, off

        def tile_of(m, off, j):
            t = 2 * m + j - off
            return t.with_bounds(min_val=0, max_val=TP - 2)

        @block.sync
        def _(sp):
            sp.dma_start(x[:], ins["in_x"]).then_inc(s_w, 16)
            for name in ONCE:
                sp.dma_start(weights[name][:], ins["in_" + name]).then_inc(s_w, 16)

            def layer_weights(names, l, sem):
                for name in names:
                    v = ins["in_" + name][ds(l, 1)]
                    v = v.rearrange("l p a b -> (l p) a b") if len(v.shape) == 4 else v.rearrange("l p a -> (l p) a")
                    sp.dma_start(weights[name][:], v).then_inc(sem, 16)

            layer_weights(["M"], 0, s_lm)
            layer_weights(LATER, 0, s_lw)
            for name, tile in lists.items():
                sp.dma_start(tile[:], ins[name]).then_inc(s_lists, 16)
            sp.dma_start(rows_i[0:NCH, :], ins["in_dst_rows"]).then_inc(s_lists, 16)
            sp.dma_start(prev_i[0:NCH, :], ins["in_dst_prev"]).then_inc(s_lists, 16)
            sp.dma_start(we[:], ins["in_We"]).then_inc(s_we, 16)
            sp.wait_ge(s_mask, 1)
            sp.dma_start(mask_dram, mask_rows[0:NCH].rearrange("p s e -> p (s e)")).then_inc(s_mask_out, 16)
            sp.wait_ge(s_ranges, 1)
            sp.wait_ge(s_prime, 1)
            with sp.Fori(0, NB) as b:
                lo, hi, off = load_pairs(sp, b)
                with sp.Fori(lo, hi) as m:
                    sp.wait_ge(s_attr_now, m + 1)
                    sp.wait_ge(s_attr, 16 * m + 16)
                    sp.dma_start(attr_ring[:, ds(m % 4, 1), :],
                                 ins["in_attrT"][:, ds(tile_of(m, off, 0) * P, 2 * P)]).then_inc(s_attr, 16)
            total = sp.value_load(ranges[0:1, NB:NB + 1], min_val=1, max_val=NB * TD)
            for k in range(2):
                last = sp.snap(total + k)
                sp.wait_ge(s_prime, 1)
                sp.wait_ge(s_attr_now, last + 1)
                sp.wait_ge(s_attr, 16 * last + 16)
                sp.dma_start(attr_ring[:, ds(last % 4, 1), :], ins["in_attrT"][:, 0:2 * P]).then_inc(s_attr, 16)

            def counts(c, n, base):
                sp.wait_ge(s_spmm, NB * c + 3)
                sp.sem_inc(s_past, 1)
                flag = sp.value_load(overflow[0:1, 0:1], min_val=0, max_val=1)

                def load(b, slot, turn):
                    sp.wait_ge(s_prime, 1)
                    sp.wait_ge(s_spmm, NB * c + b + (4 - n))
                    sp.dma_start(slab[slot][:], at_part[0][ds(b, 1)].rearrange("a p n -> (a p) n")).then_inc(
                        s_slab[slot], 16)
                    with sp.If(flag > 0):
                        sp.wait_ge(s_prime, 1)
                        sp.wait_ge(s_rest_used, NB * c + b + 1)
                        sp.dma_start(slab_rest[:], at_part[1][ds(b, 1)].rearrange("a p n -> (a p) n")).then_inc(
                            s_slab_rest, 16)
                return load

            sp.wait_ge(s_flag, 2)
            sp.wait_ge(s_store0, 16 * NB + 16)
            sp.wait_ge(s_store1, 16 * NB)
            sp.wait_ge(s_mask_out, 16)
            for c in range(5):
                in_turn(sp, 3, counts(c, 3, 0))
            sp.wait_ge(s_rows, V_X3)
            sp.dma_start(x3_dram, x[:]).then_inc(s_x3, 16)
            sp.wait_ge(s_x3, 16)
            with sp.Fori(0, LAYERS) as l:
                sp.wait_ge(s_prime, 1)
                sp.wait_ge(s_rows, V_LAYER * l + V_X3 + 1)
                sp.dma_start(a_dram.rearrange("(b p) f -> p b f", p=P), g[:]).then_inc(s_a_out, 16)
                layer_weights(["M"], (l + 1) % LAYERS, s_lm)
                load = counts(l + 5, 2, 0)

                def block_loads(b, slot, turn):
                    load(b, slot, turn)
                    for q in range(QT):
                        c = QT * b + q
                        sp.wait_ge(s_prime, 1)
                        sp.wait_ge(s_scan, NCH * l + c + 1)
                        sp.dma_start(marks[q % 2][:],
                                     mask_dram[ds(c, 1), :].rearrange("a e -> (a e)").partition_broadcast(P)
                                     ).then_inc(s_mk[q % 2], 16)
                in_turn(sp, 2, block_loads)
                sp.wait_ge(s_prime, 1)
                sp.wait_ge(s_y, NG * l + NG)
                layer_weights(LATER, (l + 1) % LAYERS, s_lw)
            sp.wait_ge(s_grp, NG * LAYERS + NG)
            sp.dma_start(g[:], x3_dram).then_inc(s_x3, 16)
            sp.wait_ge(s_rows, V_X3 + V_LAYER * LAYERS + 2)
            sp.dma_start(out[0:(NB - 1) * P, :].rearrange("(b p) f -> p b f", p=P), x[:, 0:NB - 1, :]).then_inc(
                s_out, 16)
            sp.dma_start(out[(NB - 1) * P:N, :], x[0:N - (NB - 1) * P, NB - 1, :]).then_inc(s_out, 16)
            sp.wait_ge(s_lm, 16 * (LAYERS + 1))
            sp.wait_ge(s_lw, 16 * len(LATER) * (LAYERS + 1))
            sp.wait_ge(s_out, 32)

        @block.gpsimd
        def _(pool):
            pool.sem_inc(s_ef_mm, 1)
            pool.sem_inc(s_ef_lo, 1)
            pool.sem_inc(s_ef_r1, 1)
            pool.sem_inc(s_ef32, 1)
            pool.sem_inc(s_attr_now, 4)
            pool.sem_inc(s_part0, 1)
            pool.sem_inc(s_attr, 16)
            pool.sem_inc(s_tile, 4)
            pool.sem_inc(s_ev_act, 1)
            pool.sem_inc(s_ev_dve, 1)
            pool.sem_inc(s_part1, 1)
            pool.sem_inc(s_most, 1)
            pool.sem_inc(s_store0, 16)
            pool.sem_inc(s_oh_sum, 7)
            pool.sem_inc(s_rest_used, 1)
            pool.sem_inc(s_spmm, 3)
            pool.sem_inc(s_agg, 3)
            pool.sem_inc(s_fwd, 4)
            pool.sem_inc(s_scan, 2)
            pool.sem_inc(s_back, 2)
            pool.sem_inc(s_rr, 1)
            pool.sem_inc(s_ut, 2)
            pool.sem_inc(s_grp, NG)
            pool.sem_inc(s_st[0], 16)
            pool.sem_inc(s_st[1], 16)
            pool.sem_inc(s_prime, 1)
            nc.gpsimd.memset(far_row[:, 0:D], FAR)
            nc.gpsimd.memset(far_row[:, D:2 * D], -FAR)
            nc.gpsimd.memset(eps[:, 0:1], BN_EPS)
            nc.gpsimd.memset(eps[:, 1:2], 1e-30)
            nc.gpsimd.memset(total_f[:], 0.0)
            nc.gpsimd.memset(ones[:], 1.0).then_inc(s_node, 1)
            pool.wait_ge(s_node, 1)
            nc.gpsimd.affine_select(out=upto[:], in_=ones[:], compare_op=ALU.is_ge, fill=0.0, base=0,
                                    pattern=[[1, P]], channel_multiplier=-1).then_inc(s_node, 1)
            nc.gpsimd.iota(iota_src[:], [[1, NP]], base=-MID, channel_multiplier=0,
                           allow_small_or_imprecise_dtypes=True).then_inc(s_const, 1)
            nc.gpsimd.iota(iota_dst[:], [[1, P]], base=0, channel_multiplier=0,
                           allow_small_or_imprecise_dtypes=True).then_inc(s_const, 1)
            nc.gpsimd.iota(block_base[:], [[P, NB + 1]], base=0, channel_multiplier=0,
                           allow_small_or_imprecise_dtypes=True).then_inc(s_const, 1)
            nc.gpsimd.iota(t_next[:], [[1, QT]], base=1, channel_multiplier=QT,
                           allow_small_or_imprecise_dtypes=True).then_inc(s_const, 1)
            nc.gpsimd.memset(zeros[:], 0.0).then_inc(s_const, 1)
            nc.gpsimd.memset(ones_col[:], 1.0).then_inc(s_const, 1)
            nc.gpsimd.memset(onehot_sum[:], 0.0).then_inc(s_const, 1)
            nc.gpsimd.memset(a_part[0][:], 0.0).then_inc(s_const, 1)
            nc.gpsimd.memset(identity[:], 0.0).then_inc(s_const, 1)
            pool.wait_ge(s_const, 9)
            nc.gpsimd.affine_select(out=identity[:], in_=identity[:], compare_op=ALU.not_equal, fill=1.0,
                                    base=0, pattern=[[-1, P]], channel_multiplier=1).then_inc(s_const, 1)
            pool.wait_ge(s_reach, 1)
            nc.gpsimd.partition_all_reduce(reach_all[:].rearrange("p a b -> p (a b)"),
                                           reach[:].rearrange("p a b -> p (a b)"), P, RMAX).then_inc(s_reached, 1)
            def add_rows(m):
                for j in range(2):
                    pool.wait_ge(s_const, N_CONST)
                    pool.wait_ge(s_oh, 2 * m + (j + 1))
                    pool.wait_ge(s_oh_sum, 2 * m + (7 + j))
                    nc.gpsimd.tensor_tensor(onehot_sum[:], onehot_sum[:],
                                            onehot_dst[:, ds(m % 4, 1), j, :].rearrange("p a n -> p (a n)"),
                                            ALU.add).then_inc(s_oh_sum, 1)

            def second_part(b):
                pool.wait_ge(s_const, N_CONST)
                pool.wait_ge(s_part0, b + 2)
                nc.gpsimd.tensor_tensor(a_part[1][:], a32[:], a_part[0][:], ALU.subtract).then_inc(s_part1, 1)
                pool.wait_ge(s_const, N_CONST)
                pool.wait_ge(s_part1, b + 2)
                nc.gpsimd.dma_start(at_part[1][ds(b, 1)].rearrange("a p n -> (a p) n"),
                                    a_part[1][:]).then_inc(s_store1, 16)

            pool.wait_ge(s_ranges, 1)
            add_rows(pool.snap(pool.value_load(ranges[0:1, 0:1], min_val=0, max_val=1)))
            with pool.Fori(0, NB) as b:
                lo, hi, off = load_pairs(pool, b)
                add_rows(lo + 1)
                with pool.If(b > 0):
                    second_part((b - 1).with_bounds(min_val=0, max_val=NB - 1))
                with pool.Fori(lo + 2, hi) as m:
                    add_rows(m)
                pool.wait_ge(s_const, N_CONST)
                pool.wait_ge(s_deg_mm, b + 1)
                add_rows(hi)
                with pool.If(b > 0):
                    pool.wait_ge(s_const, N_CONST)
                    pool.wait_ge(s_store1, 16 * b)
            last = pool.snap(pool.value_load(ranges[0:1, 0:1], min_val=0, max_val=1) + (NB - 1)).with_bounds(min_val=0, max_val=NB - 1)
            second_part(last)
            pool.wait_ge(s_most, NB + 3)
            nc.gpsimd.partition_all_reduce(most[:, 1:2], most[:, 0:1], P, RMAX).then_inc(s_flag, 1)

            pool.wait_ge(s_flag, 2)
            nc.gpsimd.memset(runs[1][:], 0.0).then_inc(s_node, 1)
            with pool.Fori(0, LAYERS) as l:
                pool.wait_ge(s_a_out, 16 * l + 16)
                pool.sem_inc(s_past, 1)
                with pool.Fori(0, NB) as b:
                    for q in range(QT):
                        c = NCH * l + QT * b + q
                        pool.wait_ge(s_prime, 1)
                        pool.wait_ge(s_fwd, c + 1)
                        nc.gpsimd.tensor_copy(idx_now[:, q, :], src_col[:, ds((QT * b + q) * QT, QT)]).then_inc(
                            s_idx, 1)
                        pool.wait_ge(s_prime, 1)
                        pool.wait_ge(s_idx, c + 1)
                        for t in range(QT):
                            nc.gpsimd.indirect_dma_start(
                                rows_g[:, q, t, :], None, a_dram,
                                bass.IndirectOffsetOnAxis(ap=idx_now[:, q, t:t + 1], axis=0),
                                bounds_check=NP - 1, oob_is_err=False).then_inc(s_gat[q], 16)
                pool.wait_ge(s_prime, 1)
                for i in range(2):
                    pool.wait_ge(s_st[i], 16 * (NCH // 2) * l + 16 * (NCH // 2) + 16)
                pool.wait_ge(s_spmm, NB * l + NB * 6 + 3)
                pool.sem_inc(s_past, 1)
                for b in range(NB):
                    nc.gpsimd.indirect_dma_start(
                        ends[:, b, :, :].rearrange("p s f -> p (s f)"), None, scan_dram,
                        bass.IndirectOffsetOnAxis(ap=end_idx[:, b:b + 1], axis=0),
                        bounds_check=NCH * CH, oob_is_err=False).then_inc(s_ends[b // GB], 16)

        @block.vector
        def _(dve):
            made = [0]

            def step(ins_):
                made[0] += 1
                ins_.then_inc(s_dve, 1)
                dve.wait_ge(s_dve, made[0])

            dve.wait_ge(s_lists, 64)
            dve.wait_ge(s_const, N_CONST)
            nc.vector.tensor_scalar(src_off[:], src_col[:], -float(MID), None, ALU.add)
            nc.vector.tensor_copy(dst_f[:], dst_col[:]).then_inc(s_casts, 1)
            nc.vector.tensor_copy(prev_f[0:NCH, :], prev_i[0:NCH, :])
            step(nc.vector.tensor_copy(rows_f[0:NCH, :], rows_i[0:NCH, :]))
            step(nc.vector.tensor_tensor(prev_f[0:NCH, :], rows_f[0:NCH, :], prev_f[0:NCH, :], ALU.is_equal))
            step(nc.vector.tensor_scalar(prev_f[0:NCH, :], prev_f[0:NCH, :], -1.0, 1.0, ALU.mult, ALU.add))
            nc.vector.tensor_scalar(mask_rows[0:NCH, 0, :], prev_f[0:NCH, :], -MARK, None, ALU.mult)
            nc.vector.tensor_scalar(mask_rows[0:NCH, 1, :], prev_f[0:NCH, :], 2 * MARK, -MARK, ALU.mult,
                                    ALU.add).then_inc(s_mask, 1)
            rows = rows_f[0:EQ, :].rearrange("q (j e) -> q j e", j=QT)
            nc.vector.tensor_reduce(t_min[0:EQ, :], rows, AX.X, ALU.min)
            nc.vector.tensor_reduce(t_max[0:EQ, :], rows, AX.X, ALU.max)
            nc.vector.tensor_scalar(t_left[:], t_next[:], -1.0, BIG + 1, ALU.mult, ALU.add)
            nc.vector.tensor_copy(b_lo[:], block_base[:, 0:NB])
            nc.vector.tensor_scalar(b_hi[:], block_base[:, 0:NB], float(P - 1), None, ALU.add)
            step(nc.vector.memset(reach[:], 0.0))
            for j in range(QT):
                c = slice(j, j + 1)
                step(nc.vector.tensor_scalar(touch[0:EQ, 0, :], b_hi[0:EQ, :], t_min[0:EQ, c], None, ALU.is_ge))
                step(nc.vector.scalar_tensor_tensor(touch[0:EQ, 1, :], b_lo[0:EQ, :], t_max[0:EQ, c],
                                                    touch[0:EQ, 0, :], ALU.is_le, ALU.mult))
                for k, t in enumerate((t_left, t_next)):
                    step(nc.vector.scalar_tensor_tensor(reach[0:EQ, k, :], touch[0:EQ, 1, :], t[0:EQ, c],
                                                        reach[0:EQ, k, :], ALU.mult, ALU.max))
            nc.vector.memset(rng_f[:], 0.0)
            nc.vector.memset(first[:], 0.0)
            step(nc.vector.memset(end[:], 0.0))
            dve.wait_ge(s_dve, made[0])
            nc.vector.memset(steps[:], 0.0).then_inc(s_reach, 1)
            dve.wait_ge(s_reached, 1)
            step(nc.vector.tensor_tensor_scan(end[:, 1:NB + 1], reach_all[:, 1, :], reach_all[:, 1, :], 0.0,
                                              ALU.max, ALU.max))
            step(nc.vector.tensor_scalar(first[:, 0:NB], reach_all[:, 0, :], -1.0, BIG, ALU.mult, ALU.add))
            step(nc.vector.tensor_tensor(first[:, 0:NB], first[:, 0:NB], end[:, 0:NB], ALU.min))
            step(nc.vector.tensor_tensor(steps[:], end[:, 1:NB + 1], first[:, 0:NB], ALU.subtract))
            step(nc.vector.tensor_scalar(steps[:], steps[:], 0.5, 0.25, ALU.mult, ALU.add))
            step(nc.vector.tensor_scalar(steps[:], steps[:], ROUND, None, ALU.add))
            step(nc.vector.tensor_scalar(steps[:], steps[:], -ROUND, 3.0, ALU.add, ALU.max))
            step(nc.vector.tensor_tensor_scan(rng_f[:, 1:NB + 1], steps[:], steps[:], 0.0, ALU.add, ALU.max))
            step(nc.vector.scalar_tensor_tensor(rng_f[:, 32:33 + NB], rng_f[:, 0:NB + 1], 2.0, first[:],
                                                ALU.mult, ALU.subtract))
            nc.vector.tensor_copy(ranges[:], rng_f[:]).then_inc(s_ranges, 1)
            nc.vector.memset(deg_to[:], 0.0)
            step(nc.vector.memset(a_most[:], 0.0))
            dve.wait_ge(s_ranges, 1)

            def one_hots(j, m, b, off):
                t = tile_of(m, off, j)
                parts = ef_split[:, ds(m % 2, 1), :, :].rearrange("p a j f -> p (a j) f")
                if j == 0:
                    dve.wait_ge(s_ef_lo, m + 1)
                    dve.wait_ge(s_ef_hi, m + 1)
                    nc.vector.tensor_tensor(ef_rest[:], ef32[:], parts[:, :, 0:D], ALU.subtract).then_inc(s_ef_r1, 1)
                dve.wait_ge(s_tile, 2 * m + (j + 3))
                dve.wait_ge(s_oh_sum, 2 * m + (j + 1))
                nc.vector.tensor_scalar(onehot_src[:, j, :], iota_src[:], src_off[:, ds(t, 1)], None, ALU.is_equal)
                nc.vector.tensor_scalar(onehot_dst[:, ds(m % 4, 1), j, :].rearrange("p a n -> p (a n)"), iota_dst[:], block_base[:, ds(b, 1)],
                                        dst_f[:, ds(t, 1)], ALU.add,
                                        ALU.is_equal).then_inc(s_oh, 1)
                if j == 0:
                    dve.wait_ge(s_ef_mid, m + 1)
                    nc.vector.tensor_tensor(parts[:, :, 2 * D:3 * D], ef_rest[:], parts[:, :, D:2 * D],
                                            ALU.subtract).then_inc(s_ef_lo, 1)

            def largest(b):
                dve.wait_ge(s_part0, b + 1)
                dve.wait_ge(s_most, b + 1)
                nc.vector.tensor_tensor(a_most[:], a_most[:], a_part[0][:], ALU.max).then_inc(s_most, 1)

            off0 = dve.value_load(ranges[0:1, 32:33], min_val=0, max_val=2 * NB * TD)
            zero = dve.snap(dve.value_load(ranges[0:1, 0:1], min_val=0, max_val=1))
            one_hots(0, zero, 0, off0)
            one_hots(1, zero, 0, off0)
            with dve.Fori(0, NB) as b:
                lo, hi, off = load_pairs(dve, b)
                with dve.Fori(lo + 1, hi) as m:
                    one_hots(0, m, b, off)
                    one_hots(1, m, b, off)
                largest(b)
                off_next = dve.value_load(ranges[0:1, ds(b + 33, 1)], min_val=0, max_val=2 * NB * TD)
                one_hots(0, hi, b + 1, off_next)
                dve.wait_ge(s_block, b + 1)
                dve.wait_ge(s_part1, b + 1)
                nc.vector.tensor_copy(a32[:, 2048:ACC], psum[:, 2048:ACC])
                nc.vector.tensor_reduce(edge_sum[:, ds(b, 1), :].rearrange("p a f -> p (a f)"),
                                        psum[:, ACC:ACC + 3 * D].rearrange("p (s f) -> p f s", s=3),
                                        AX.X, ALU.add)
                dve.wait_ge(s_deg_mm, b + 1)
                nc.vector.tensor_copy(deg_to[:, ds(b + 1, 1)], psum[:, 0:1]).then_inc(s_ev_dve, 1)
                one_hots(1, hi, b + 1, off_next)
            largest(NB)
            dve.wait_ge(s_ev_dve, NB + 1)
            nc.vector.tensor_tensor(deg[:], deg_to[:, 1:NB + 1], deg_to[:, 0:NB], ALU.subtract)
            dve.wait_ge(s_most, NB + 2)
            nc.vector.tensor_reduce(most[:, 0:1], a_most[:], AX.X, ALU.max).then_inc(s_most, 1)
            dve.wait_ge(s_flag, 1)
            nc.vector.tensor_scalar(overflow[:], most[:, 1:2], 256.0, None, ALU.is_ge).then_inc(s_flag, 1)


            V = nc.vector
            dve.wait_ge(s_store0, 16 * NB + 16)
            dve.wait_ge(s_store1, 16 * NB)

            def blk(tile, b):
                return tile[:, b, :] if len(tile.shape) == 3 else tile[:, b * P:(b + 1) * P]

            def flat(tile):
                return tile[:].rearrange("p b f -> p (b f)")

            def across(row):
                return row.unsqueeze(1).to_broadcast([P, NB, D])

            def scaled(tile, source, col):
                for b in range(NB):
                    last = V.tensor_scalar(tile[:, b, :], source[:, b, :], col[:, b:b + 1], None, ALU.mult)
                return last

            def split(n, source, at):
                for i in range(5):
                    five = slice(5 * i, 5 * i + 5)
                    dve.wait_ge(s_hi, 5 * n + (i + 1))
                    V.tensor_tensor(agg[:, five, :], source[:, five, :], hs[:, five, at, :],
                                    ALU.subtract).then_inc(s_r1, 1)
                for i in range(5):
                    five = slice(5 * i, 5 * i + 5)
                    dve.wait_ge(s_mid, 5 * n + (i + 1))
                    V.tensor_tensor(hs[:, five, at + 2, :], agg[:, five, :], hs[:, five, at + 1, :],
                                    ALU.subtract).then_inc(s_hs, 1)
                dve.wait_ge(s_hs, 5 * n + 5)

            def gather_sums(c):
                def take(b, slot, turn):
                    dve.wait_ge(s_spmm, NB * c + b + 4)
                    V.tensor_reduce(agg[:, ds(b, 1), :].rearrange("p a f -> p (a f)"),
                                    bank(slot)[:, 0:3 * D].rearrange("p (s f) -> p f s", s=3),
                                    AX.X, ALU.add).then_inc(s_agg, 1)
                in_turn(dve, 3, take)
                dve.wait_ge(s_agg, NB * c + NB + 3)

            def layer_norm(source, stds):
                for b in range(NB):
                    last = V.bn_stats(stats[:, b, :], source[:, b, :])
                step(last)
                for b in range(NB):
                    last = V.bn_aggr(mv[:, b, :], stats[:, b, :])
                last.then_inc(s_rows, 1)
                dve.wait_ge(s_std, stds)
                step(V.reciprocal(rstd[:], std[:]))

            def normalized(target, source):
                for b in range(NB):
                    last = V.tensor_scalar(target[:, b, :], source[:, b, :], mv[:, b, 0:1], rstd[:, b:b + 1],
                                           ALU.subtract, ALU.mult)
                return last

            def batch_norm(source, gamma, beta, stds):
                for i in range(7):
                    last = V.bn_stats(cstats[:, i, :], source[:, i * 512:min(N, (i + 1) * 512)])
                step(last)
                V.bn_aggr(cmv[:], cstats[:].rearrange("p a b -> p (a b)")).then_inc(s_rows, 1)
                dve.wait_ge(s_std, stds)
                step(V.reciprocal(cscale[:], cstd[:]))
                step(V.tensor_tensor(cscale[:], cscale[:], gamma, ALU.mult))
                step(V.tensor_tensor(cshift[:], cmv[:, 0:1], cscale[:], ALU.mult))
                V.tensor_tensor(cshift[:], beta, cshift[:], ALU.subtract).then_inc(s_rows, 1)

            def results(base, n, take):
                for b in range(n):
                    dve.wait_ge(s_mm, base + (b + 1))
                    take(b, bank(4 + b % 2)).then_inc(s_res, 1)

            step(V.tensor_scalar(d_self[:], deg[:], 1.0, None, ALU.add))
            V.tensor_copy(some[:], deg[:]).then_inc(s_rows, 1)
            cols, rows3 = weights["L1_cols"], weights["rows"]
            dve.wait_ge(s_w, 16 * (1 + len(ONCE)))
            V.tensor_scalar(one_eps[:], cols[:, 6:7], 1.0, None, ALU.add)
            dve.wait_ge(s_node, 2)
            dve.wait_ge(s_rank, 1)
            V.tensor_copy(end_f[:], bank(0)[:, 0:NB])
            step(V.tensor_copy(std[:], bank(1)[:, 0:NB]))
            step(V.tensor_tensor_scan(total_f[:, 1:NB + 1], std[:], std[:], 0.0, ALU.add, ALU.max))
            step(V.tensor_tensor(end_f[:], end_f[:], total_f[:, 0:NB], ALU.add))
            step(V.tensor_scalar(end_f[:], end_f[:], -float(NCH * CH + 1), None, ALU.add))
            step(V.tensor_scalar(some[:], deg[:], 0.5, None, ALU.is_ge))
            step(V.tensor_tensor(end_f[:], end_f[:], some[:], ALU.mult))
            step(V.tensor_scalar(end_idx[:], end_f[:], float(NCH * CH), None, ALU.add))
            dve.wait_ge(s_std, 1)
            step(V.tensor_scalar(log4[:], log4[:], 0.25, None, ALU.mult))
            V.reciprocal(inv4[:], log4[:])
            V.reciprocal(rdeg[:], d_self[:])
            step(V.reciprocal(dinv[:], root[:]))
            scaled(g, x, dinv).then_inc(s_rows, 1)
            dve.wait_ge(s_rows, 2)
            split(0, g, 0)
            gather_sums(0)
            step(V.tensor_tensor(flat(agg), flat(agg), flat(g), ALU.add))
            scaled(agg, agg, dinv).then_inc(s_rows, 1)
            results(0, NB, lambda b, ps: V.tensor_scalar(g[:, b, :], ps[:, 0:D], dinv[:, b:b + 1], None, ALU.mult))
            dve.wait_ge(s_res, NB)
            V.tensor_copy(cstats[:, 0, 0:1], dinv[:, 0:1]).then_inc(s_rows, 1)
            split(1, g, 0)
            gather_sums(1)
            step(V.tensor_tensor(flat(agg), flat(agg), flat(g), ALU.add))
            for b in range(NB):
                last = V.scalar_tensor_tensor(agg[:, b, :], agg[:, b, :], dinv[:, b:b + 1], rows3[:, 0, :],
                                              ALU.mult, ALU.add)
            step(last)
            step(V.scalar_tensor_tensor(flat(agg), flat(agg), 0.0, flat(x), ALU.max, ALU.add))
            layer_norm(agg, 2)
            normalized(x, agg).then_inc(s_rows, 1)
            dve.wait_ge(s_rows, 6)
            split(2, x, 0)
            gather_sums(2)
            step(V.scalar_tensor_tensor(flat(agg), flat(x), one_eps[:, 0:1], flat(agg), ALU.mult, ALU.add))
            V.tensor_tensor(flat(agg), flat(agg), flat(edge_sum), ALU.add).then_inc(s_rows, 1)
            results(NB, NB, lambda b, ps: V.tensor_scalar(blk(ft, b), ps[:, 0:D], cols[:, 0:1], None, ALU.add))
            dve.wait_ge(s_res, 2 * NB)
            batch_norm(ft, cols[:, 1:2], cols[:, 2:3], 3)
            results(2 * NB, 7, lambda i, ps: V.tensor_scalar(
                ft2[:, i * 512:min(NP, (i + 1) * 512)], ps[:, 0:min(NP, (i + 1) * 512) - i * 512], cols[:, 3:4],
                None, ALU.add))
            dve.wait_ge(s_res, 2 * NB + 7)
            batch_norm(ft2, cols[:, 4:5], cols[:, 5:6], 4)
            results(2 * NB + 7, NB, lambda b, ps: V.tensor_tensor(agg[:, b, :], ps[:, 0:D], x[:, b, :], ALU.add))
            dve.wait_ge(s_res, 3 * NB + 7)
            layer_norm(agg, 5)
            normalized(x, agg).then_inc(s_rows, 1)
            dve.wait_ge(s_rows, 13)
            split(3, x, 0)
            gather_sums(3)
            step(V.tensor_tensor(flat(agg), flat(agg), flat(x), ALU.add))
            scaled(agg, agg, rdeg).then_inc(s_rows, 1)
            results(3 * NB + 7, NB, lambda b, ps: V.tensor_tensor(g[:, b, :], ps[:, 0:D], rows3[:, 1, :], ALU.add))
            dve.wait_ge(s_res, 4 * NB + 7)
            V.scalar_tensor_tensor(flat(g), flat(g), 0.01, flat(g), ALU.mult, ALU.max).then_inc(s_rows, 1)
            dve.wait_ge(s_rows, 15)
            split(4, g, 0)
            gather_sums(4)
            step(V.tensor_tensor(flat(agg), flat(agg), flat(g), ALU.add))
            scaled(agg, agg, rdeg).then_inc(s_rows, 1)
            results(4 * NB + 7, NB, lambda b, ps: V.tensor_tensor(g[:, b, :], ps[:, 0:D], rows3[:, 2, :], ALU.add))
            dve.wait_ge(s_res, 5 * NB + 7)
            step(V.tensor_tensor(flat(agg), flat(g), flat(x), ALU.add))
            layer_norm(agg, 6)
            normalized(x, agg).then_inc(s_rows, 1)
            lrows, lcols = weights["L3_rows"], weights["L3_cols"]
            at_entry = made[0]
            with dve.Fori(0, LAYERS) as l:
                def step(ins_):
                    made[0] += 1
                    ins_.then_inc(s_dve, 1)
                    dve.wait_ge(s_dve, DVE_LAYER * l + made[0])
                    dve.sem_inc(s_past, 1)

                def told(k):
                    return V_LAYER * l + V_X3 + k

                for b in range(NB):
                    dve.wait_ge(s_mm, 3 * NB * l + MM3 + (b + 1))
                    V.tensor_copy(g[:, b, :], bank(4 + b % 2)[:, 0:D]).then_inc(s_res, 1)
                dve.wait_ge(s_res, 2 * NB * l + MM3 + NB)
                V.tensor_copy(cstats[:, 0, 0:1], dinv[:, 0:1]).then_inc(s_rows, 1)
                V.tensor_tensor(ft[:], flat(g), flat(g), ALU.mult).then_inc(s_rows, 1)
                dve.wait_ge(s_rows, told(2))
                split(2 * l + 5, g, 0)
                split(2 * l + 6, ft[:].rearrange("p (b f) -> p b f", b=NB), 3)
                dve.sem_inc(s_past, 1)

                def chunks(b, slot, turn):
                    for q in range(QT):
                        c = NCH * l + QT * b + q
                        dve.wait_ge(s_mk[q % 2], 16 * (NCH // 2) * l + 32 * b + 16 * (q // 2 + 1))
                        dve.wait_ge(s_fwd, c + 5)
                        dve.wait_ge(s_back, c + 1)
                        dve.wait_ge(s_scan, c + 2)
                        dve.wait_ge(s_node, 3)
                        before = runs[(q + 1) % 2]
                        V.tensor_tensor_scan(runs[q % 2][:, 0, :], marks[q % 2][:, 0:CH], bank(q % 2),
                                             before[:, 0, CH - 1:CH], ALU.add, ALU.max)
                        V.tensor_tensor_scan(runs[q % 2][:, 1, :], marks[q % 2][:, CH:2 * CH], bank(q % 2),
                                             before[:, 1, CH - 1:CH], ALU.max, ALU.min).then_inc(s_scan, 1)
                    n = NB * l + b
                    dve.wait_ge(s_spmm, n + (NB * 5 + 4))
                    three = "p (s f) -> p f s"
                    V.tensor_reduce(var_tmp[:, 0, :], bank(4 + 2 * slot)[:, 0:3 * D].rearrange(three, s=3),
                                    AX.X, ALU.add)
                    V.tensor_reduce(var_tmp[:, 1, :], bank(5 + 2 * slot)[:, 0:3 * D].rearrange(three, s=3),
                                    AX.X, ALU.add).then_inc(s_agg, 1)
                    dve.wait_ge(s_agg, n + (NB * 5 + 4))
                    own = g[:, ds(b, 1), :].rearrange("p a f -> p (a f)")
                    V.tensor_tensor(var_tmp[:, 0, :], var_tmp[:, 0, :], own, ALU.add)
                    V.tensor_tensor(var_tmp[:, 1, :], var_tmp[:, 1, :], ft[:, ds(b * D, D)], ALU.add).then_inc(s_var, 1)
                    dve.wait_ge(s_var, 4 * n + 1)
                    V.tensor_scalar(var_tmp[:, 0:2, :], var_tmp[:, 0:2, :], rdeg[:, ds(b, 1)], None,
                                    ALU.mult).then_inc(s_var, 1)
                    dve.wait_ge(s_var, 4 * n + 2)
                    V.tensor_tensor(var_tmp[:, 2, :], var_tmp[:, 0, :], var_tmp[:, 0, :], ALU.mult).then_inc(s_var, 1)
                    dve.wait_ge(s_var, 4 * n + 3)
                    V.tensor_tensor(var_tmp[:, 3, :], var_tmp[:, 1, :], var_tmp[:, 2, :], ALU.subtract).then_inc(
                        s_var, 1)
                    dve.wait_ge(s_var, 4 * n + 4)
                    V.tensor_scalar(agg[:, ds(b, 1), :].rearrange("p a f -> p (a f)"), var_tmp[:, 3, :], 0.0, None,
                                    ALU.max)

                in_turn(dve, 2, chunks)
                step(V.tensor_copy(cstats[:, 0, 0:1], dinv[:, 0:1]))
                V.tensor_copy(cstats[:, 0, 1:2], dinv[:, 0:1]).then_inc(s_rows, 1)
                dve.wait_ge(s_ab, NB * l + NB)
                dve.wait_ge(s_lw, 16 * len(LATER) * l + 16 * len(LATER))

                def merge(i):
                    at = slice(GB * i, GB * i + GB)
                    dve.wait_ge(s_ends[i], 16 * GB * l + 16 * GB)
                    V.tensor_tensor(ends[:, at, 0, :], ends[:, at, 0, :], g[:, at, :], ALU.max)
                    step(V.tensor_tensor(ends[:, at, 1, :], ends[:, at, 1, :], g[:, at, :], ALU.min))
                    V.tensor_tensor(ends[:, at, 0, :], ends[:, at, 0, :], edge_sum[:, at, :], ALU.add)
                    V.tensor_tensor(ends[:, at, 1, :], ends[:, at, 1, :], edge_sum[:, at, :], ALU.add).then_inc(
                        s_merged, 1)

                merge(0)
                for b in range(NB):
                    if b % GB == 0 and b // GB + 1 < NG:
                        merge(b // GB + 1)
                    ps = bank(2 + b % 2)
                    u = u_row[:, b % 2, :]
                    dve.wait_ge(s_mm, 3 * NB * l + (MM3 + NB + b + 1))
                    dve.wait_ge(s_ut, NB * l + (b + 1))
                    step(V.scalar_tensor_tensor(u, ps[:, D:2 * D], log4[:, b:b + 1], blk(ft2, b), ALU.mult, ALU.add))
                    step(V.scalar_tensor_tensor(u, ps[:, 2 * D:3 * D], inv4[:, b:b + 1], u, ALU.mult, ALU.add))
                    V.tensor_tensor(u, ps[:, 0:D], u, ALU.add).then_inc(s_u, 1)
                dve.wait_ge(s_act, NB * l + NB)
                batch_norm(flat(edge_sum), lcols[:, 0:1], lcols[:, 1:2], S_LAYER * l + (S_X3 + 2))
                for i in range(NG):
                    at = slice(GB * i, GB * i + GB)
                    for b in range(GB * i, GB * i + GB):
                        dve.wait_ge(s_mm, 3 * NB * l + (MM3 + 2 * NB + b + 1))
                        V.tensor_tensor(agg[:, b, :], bank(4 + b % 2)[:, 0:D], lrows[:, 2, :], ALU.add).then_inc(
                            s_res, 1)
                    dve.wait_ge(s_res, 2 * NB * l + (MM3 + NB + GB * i + GB))
                    step(V.scalar_tensor_tensor(agg[:, at, :], agg[:, at, :], 0.01, agg[:, at, :], ALU.mult, ALU.max))
                    step(V.tensor_tensor(agg[:, at, :], agg[:, at, :], x[:, at, :], ALU.add))
                    for b in range(GB * i, GB * i + GB):
                        last = V.bn_stats(stats[:, b, :], agg[:, b, :])
                step(last)
                for b in range(NB):
                    last = V.bn_aggr(mv[:, b, :], stats[:, b, :])
                last.then_inc(s_rows, 1)
                dve.wait_ge(s_std, S_LAYER * l + (S_X3 + 3))
                step(V.reciprocal(rstd[:], std[:]))
                for i in range(NG + 1):
                    if i < NG:
                        for b in range(GB * i, GB * i + GB):
                            last = V.scalar_tensor_tensor(agg[:, b, :], agg[:, b, :], mv[:, b, 0:1], lrows[:, 3, :],
                                                          ALU.subtract, ALU.mult)
                        step(last)
                        for b in range(GB * i, GB * i + GB):
                            last = V.scalar_tensor_tensor(agg[:, b, :], agg[:, b, :], rstd[:, b:b + 1],
                                                          lrows[:, 4, :], ALU.mult, ALU.add)
                        last.then_inc(s_y, 1)
                    if i >= 1:
                        at = slice(GB * i - GB, GB * i)
                        dve.wait_ge(s_e, NG * l + i)
                        step(V.tensor_scalar(agg[:, at, :], agg[:, at, :], 0.0, -1.0, ALU.max, ALU.add))
                        V.tensor_tensor(x[:, at, :], agg[:, at, :], g[:, at, :], ALU.add).then_inc(s_grp, 1)
                dve.wait_ge(s_grp, NG * l + 2 * NG)
            assert made[0] - at_entry == DVE_LAYER, made[0] - at_entry
            made[0] += (LAYERS - 1) * DVE_LAYER

            def step(ins_):
                made[0] += 1
                ins_.then_inc(s_dve, 1)
                dve.wait_ge(s_dve, made[0])
            dve.wait_ge(s_x3, 32)
            step(V.tensor_tensor(flat(agg), flat(g), flat(x), ALU.add))
            layer_norm(agg, S_X3 + S_LAYER * LAYERS + 1)
            normalized(x, agg).then_inc(s_rows, 1)

        @block.scalar
        def _(act):
            act.wait_ge(s_ranges, 1)

            def attributes(m):
                act.wait_ge(s_attr, 16 * m + 32)
                act.wait_ge(s_ef_mm, m + 1)
                act.wait_ge(s_prime, 1)
                nc.scalar.copy(attr_now[:], attr_ring[:, ds(m % 4, 1), :].rearrange(
                    "p a b -> p (a b)")).then_inc(s_attr_now, 1)

            def edge_features(m):
                attributes(m + 1)
                act.wait_ge(s_ef_mm, m + 2)
                act.wait_ge(s_ef_r1, m + 1)
                act.wait_ge(s_prime, 1)
                nc.scalar.activation(ef32[:], psum[:, 3584:3840].rearrange("p (j f) -> p j f", j=2),
                                     ACT.Relu).then_inc(s_ef32, 1)
                act.wait_ge(s_ef32, m + 2)
                act.wait_ge(s_tile, 2 * m + 2)
                act.wait_ge(s_prime, 1)
                nc.scalar.copy(ef_split[:, ds(m % 2, 1), :, 0:D].rearrange("p a j f -> p (a j) f"),
                               ef32[:]).then_inc(s_ef_hi, 1)
                act.wait_ge(s_ef_r1, m + 2)
                act.wait_ge(s_prime, 1)
                nc.scalar.copy(ef_split[:, ds(m % 2, 1), :, D:2 * D].rearrange("p a j f -> p (a j) f"),
                               ef_rest[:]).then_inc(s_ef_mid, 1)

            zero = act.snap(act.value_load(ranges[0:1, 0:1], min_val=0, max_val=1))
            attributes(zero)
            edge_features(zero)
            def first_part(b):
                act.wait_ge(s_ev_act, b + 2)
                act.wait_ge(s_ev_dve, b + 2)
                act.wait_ge(s_most, b + 2)
                act.wait_ge(s_store0, 16 * b + 16)
                act.wait_ge(s_prime, 1)
                nc.scalar.copy(a_part[0][:], a32[:]).then_inc(s_part0, 1)
                act.wait_ge(s_part0, b + 2)
                act.wait_ge(s_prime, 1)
                act.dma_start(at_part[0][ds(b, 1)].rearrange("a p n -> (a p) n"), a_part[0][:]).then_inc(s_store0, 16)

            with act.Fori(0, NB) as b:
                lo, hi, off = load_pairs(act, b)
                edge_features(lo + 1)
                with act.If(b > 0):
                    first_part((b - 1).with_bounds(min_val=0, max_val=NB - 1))
                with act.Fori(lo + 2, hi) as m:
                    edge_features(m)
                edge_features(hi)
                act.wait_ge(s_block, b + 1)
                act.wait_ge(s_part1, b + 1)
                act.wait_ge(s_prime, 1)
                nc.scalar.copy(a32[:, 0:512], psum[:, 0:512]).then_inc(s_ev_first, 1)
                nc.scalar.copy(a32[:, 512:2048], psum[:, 512:2048]).then_inc(s_ev_act, 1)
            first_part(act.snap(act.value_load(ranges[0:1, 0:1], min_val=0, max_val=1) + (NB - 1)).with_bounds(min_val=0, max_val=NB - 1))

            A = nc.scalar

            def split(n, source, at):
                for i in range(5):
                    five = slice(5 * i, 5 * i + 5)
                    A.copy(hs[:, five, at, :], source[:, five, :]).then_inc(s_hi, 1)
                for i in range(5):
                    five = slice(5 * i, 5 * i + 5)
                    act.wait_ge(s_r1, 5 * n + (i + 1))
                    A.copy(hs[:, five, at + 1, :], agg[:, five, :]).then_inc(s_mid, 1)

            def turned_blocks(trs, trcs, mms, width):
                for b in range(NB):
                    act.wait_ge(s_tr, trs + (b + 1))
                    if b >= 2:
                        act.wait_ge(s_mm, mms + (b - 1))
                    A.copy(turned[:, b % 2, 0:width], bank(b % 2)[:, 0:width]).then_inc(s_trc, 1)

            def root_of(rows, target, source, e):
                act.wait_ge(s_rows, rows)
                A.activation(target, source, ACT.Sqrt, bias=eps[:, e:e + 1]).then_inc(s_std, 1)

            act.wait_ge(s_flag, 2)
            act.dma_start(scan_dram[NCH * CH:NCH * CH + 1, :], far_row[:]).then_inc(s_far, 16)
            act.wait_ge(s_rows, 1)
            A.activation(log4[:], d_self[:], ACT.Ln, bias=ones[:, 0:1])
            A.activation(root[:], d_self[:], ACT.Sqrt).then_inc(s_std, 1)
            act.wait_ge(s_rows, 2)
            split(0, g, 0)
            cols = weights["L1_cols"]
            for i in range(NB + 1):
                if i < NB:
                    act.wait_ge(s_tr, i + 1)
                    if i >= 2:
                        act.wait_ge(s_hid, i - 1)
                    A.copy(turned[:, i % 2, 0:D], bank(i % 2)[:, 0:D]).then_inc(s_trc, 1)
                if i >= 1:
                    b = i - 1
                    act.wait_ge(s_hid, b + 1)
                    if b >= 2:
                        act.wait_ge(s_mm, b - 1)
                    for k in range(HC):
                        last = A.activation(hidden[:, b % 2, k, :], bank(2 + b % 2)[:, k * P:(k + 1) * P], ACT.Relu,
                                            bias=weights["L0_b1"][:, k:k + 1])
                    last.then_inc(s_hidr, 1)
            act.wait_ge(s_rows, 4)
            split(1, g, 0)
            root_of(5, std[:], mv[:, :, 1], 0)
            act.wait_ge(s_rows, 6)
            split(2, x, 0)
            turned_blocks(NB, NB, NB, D)
            root_of(8, cstd[:], cmv[:, 1:2], 0)
            act.wait_ge(s_rows, 9)
            for i in range(7):
                c = slice(i * 512, min(NP, (i + 1) * 512))
                A.activation(ft[:, c], ft[:, c], ACT.Relu, bias=cshift[:, 0:1], scale=cscale[:, 0:1]).then_inc(s_z, 1)
            root_of(10, cstd[:], cmv[:, 1:2], 0)
            act.wait_ge(s_rows, 11)
            for b in range(NB):
                if b >= 2:
                    act.wait_ge(s_mm, 2 * NB + 7 + b - 1)
                A.activation(turned[:, b % 2, 0:D], ft2[:, b * P:(b + 1) * P], ACT.Relu, bias=cshift[:, 0:1],
                             scale=cscale[:, 0:1]).then_inc(s_trc, 1)
            root_of(12, std[:], mv[:, :, 1], 0)
            act.wait_ge(s_rows, 13)
            split(3, x, 0)
            turned_blocks(2 * NB, 3 * NB, 3 * NB + 7, D)
            act.wait_ge(s_rows, 15)
            split(4, g, 0)
            turned_blocks(3 * NB, 4 * NB, 4 * NB + 7, D)
            root_of(17, std[:], mv[:, :, 1], 0)
            act.wait_ge(s_far, 16)
            with act.Fori(0, LAYERS) as l:
                def told(k):
                    return V_LAYER * l + V_X3 + k

                mms = 3 * NB * l + MM3
                for i in range(NB + 1):
                    if i < NB:
                        act.wait_ge(s_tr, 2 * NB * l + 4 * NB + (i + 1))
                        if i >= 2:
                            act.wait_ge(s_mm, mms + (i - 1))
                        A.copy(turned[:, i % 2, 0:D], bank(i % 2)[:, 0:D]).then_inc(s_trc, 1)
                    if i >= 1:
                        b = i - 1
                        act.wait_ge(s_mm, mms + (b + 1))
                        A.copy(edge_sum[:, b, :], bank(6 + b % 2)[:, 0:D])
                        A.copy(ft2[:, b * P:(b + 1) * P], bank(6 + b % 2)[:, D:2 * D]).then_inc(s_ab, 1)
                act.wait_ge(s_rows, told(2))
                split(2 * l + 5, g, 0)
                split(2 * l + 6, ft[:].rearrange("p (b f) -> p b f", b=NB), 3)
                with act.Fori(0, NB) as b:
                    for q in range(QT):
                        c = NCH * l + QT * b + q
                        act.wait_ge(s_back, c + 3)
                        act.wait_ge(s_st[q % 2], 16 * (NCH // 2) * l + 32 * b + 16 * (q // 2 + 1))
                        act.wait_ge(s_prime, 1)
                        A.copy(run_rows[q % 2][:].rearrange("p t f -> p (t f)"), psum[:, 1024:2048]).then_inc(s_rr, 1)
                        act.wait_ge(s_rr, c + 2)
                        act.wait_ge(s_prime, 1)
                        act.dma_start(scan_dram[ds((QT * b + q) * CH, CH), :].rearrange("(t p) f -> p t f", p=P),
                                      run_rows[q % 2][:]).then_inc(s_st[q % 2], 16)
                act.wait_ge(s_rows, told(3))
                A.activation(ft[:], agg[:].rearrange("p b f -> p (b f)"), ACT.Sqrt, bias=eps[:, 1:2]).then_inc(s_std, 1)
                for i in range(NB + 2):
                    if i < NB:
                        act.wait_ge(s_tr, 2 * NB * l + (5 * NB + i + 1))
                        if i >= 2:
                            act.wait_ge(s_mm, mms + (NB + i - 1))
                        A.copy(turned[:, i % 2, :], bank(i % 2)[:, :]).then_inc(s_trc, 1)
                    if i >= 2:
                        b = i - 2
                        act.wait_ge(s_ut, NB * l + (b + 3))
                        A.mul(edge_sum[:, b, :], bank(4 + b % 2)[:, 0:D], float(np.sqrt(np.float32(1.0 / N)))).then_inc(
                            s_act, 1)
                root_of(told(4), cstd[:], cmv[:, 1:2], 0)
                act.wait_ge(s_rows, told(5))
                for b in range(NB):
                    if b >= 2:
                        act.wait_ge(s_mm, mms + (2 * NB + b - 1))
                    A.activation(turned[:, b % 2, 0:D], edge_sum[:, b, :], ACT.Identity, bias=cshift[:, 0:1],
                                 scale=cscale[:, 0:1]).then_inc(s_trc, 1)
                root_of(told(6), std[:], mv[:, :, 1], 0)
                for i in range(NG):
                    at = slice(GB * i, GB * i + GB)
                    act.wait_ge(s_y, NG * l + (i + 1))
                    A.activation(g[:, at, :], agg[:, at, :], ACT.Relu, scale=-1.0).then_inc(s_neg, 1)
                    act.wait_ge(s_neg, NG * l + (i + 1))
                    A.activation(g[:, at, :], g[:, at, :], ACT.Exp, scale=-1.0).then_inc(s_e, 1)
            root_of(V_X3 + V_LAYER * LAYERS + 1, std[:], mv[:, :, 1], 0)

        @block.tensor
        def _(pe):
            def edge_features(m):
                pe.wait_ge(s_attr_now, m + 5)
                pe.wait_ge(s_ef32, m + 1)
                for j in range(2):
                    mm = nc.tensor.matmul(psum[:, 3584 + j * D:3584 + (j + 1) * D], attr_now[:, j * P:(j + 1) * P],
                                          we[:], start=True, stop=True)
                mm.then_inc(s_ef_mm, 1)

            pe.wait_ge(s_const, N_CONST)
            pe.wait_ge(s_we, 16)
            pe.wait_ge(s_ranges, 1)
            zero = pe.snap(pe.value_load(ranges[0:1, 0:1], min_val=0, max_val=1))
            edge_features(zero)
            edge_features(zero + 1)
            with pe.Fori(0, NB) as b:
                lo, hi, off = load_pairs(pe, b)
                pe.wait_ge(s_ev_act, b + 1)
                pe.wait_ge(s_ev_dve, b + 1)
                for k in range(7):
                    nc.tensor.matmul(psum[:, k * 512:k * 512 + 1], zeros[:, 0:P], zeros[:, 0:1], start=True,
                                     stop=False, skip_group_check=True)
                with pe.Fori(lo, hi) as m:
                    for j in range(2):
                        rows = onehot_dst[:, ds(m % 4, 1), j, :].rearrange("p a n -> p (a n)")
                        pe.wait_ge(s_oh, 2 * m + (j + 1))
                        for k in range(NB):
                            nc.tensor.matmul(psum[:, k * P:(k + 1) * P],
                                             onehot_src[:, j, k * P:(k + 1) * P], rows, start=False, stop=False,
                                             skip_group_check=True)
                        if j == 0:
                            pe.wait_ge(s_ef_lo, m + 2)
                        nc.tensor.matmul(psum[:, ACC:ACC + 3 * D], rows,
                                         ef_split[:, ds(m % 2, 1), j, :].rearrange("p a f -> p (a f)"),
                                         start=False, stop=False, skip_group_check=True).then_inc(s_tile, 1)
                        if j == 0:
                            edge_features(m + 2)
                for k in range(7):
                    mm = nc.tensor.matmul(psum[:, k * 512:k * 512 + 1], zeros[:, 0:P], zeros[:, 0:1], start=False,
                                          stop=True, skip_group_check=True)
                mm.then_inc(s_block, 1)
                pe.wait_ge(s_oh_sum, 2 * hi + 7)
                pe.wait_ge(s_ev_first, b + 1)
                nc.tensor.matmul(psum[:, 0:1], onehot_sum[:], ones_col[:], start=True, stop=True,
                                 skip_group_check=True).then_inc(s_deg_mm, 1)


            T = nc.tensor

            def sums(c, n):
                flag = pe.value_load(overflow[0:1, 0:1], min_val=0, max_val=1)

                def one(b, slot, turn):
                    pe.wait_ge(s_slab[slot], 16 * (SLABS[slot] * c + turn) + 16)
                    pe.wait_ge(s_agg, NB * c + b + 1)
                    count_products(pe, [bank(slot)], [0], slab[slot], range(NB - 1), flag, c, b)
                return one

            def count_products(pe, banks, ats, counts, ks, flag, c, b):
                for k in ks:
                    for ps, at in zip(banks, ats):
                        T.matmul(ps[:, 0:3 * D], counts[:, k * P:(k + 1) * P],
                                 hs[:, k, at:at + 3, :].rearrange("p s f -> p (s f)"), start=(k == 0), stop=False,
                                 skip_group_check=True)
                with pe.If(flag > 0):
                    pe.wait_ge(s_prime, 1)
                    pe.wait_ge(s_slab_rest, 16 * (NB * c + b) + 16)
                    for k in range(NB):
                        for ps, at in zip(banks, ats):
                            mm = T.matmul(ps[:, 0:3 * D], slab_rest[:, k * P:(k + 1) * P],
                                          hs[:, k, at:at + 3, :].rearrange("p s f -> p (s f)"), start=False,
                                          stop=False, skip_group_check=True)
                    mm.then_inc(s_rest_used, 1)
                k = NB - 1
                for ps, at in zip(banks, ats):
                    mm = T.matmul(ps[:, 0:3 * D], counts[:, k * P:(k + 1) * P],
                                  hs[:, k, at:at + 3, :].rearrange("p s f -> p (s f)"), start=False, stop=True,
                                  skip_group_check=True)
                mm.then_inc(s_spmm, 1)

            def turn(b, source, trcs):
                if b >= 2:
                    pe.wait_ge(s_trc, trcs + (b - 1))
                T.transpose(bank(b % 2)[:, 0:P], source[:, b, :], identity[:]).then_inc(s_tr, 1)

            def turned_products(source, trcs, ress, product):
                for i in range(NB + 1):
                    if i < NB and source is not None:
                        turn(i, source, trcs)
                    if i >= 1:
                        b = i - 1
                        pe.wait_ge(s_trc, trcs + (b + 1))
                        if b >= 2:
                            pe.wait_ge(s_res, ress + (b - 1))
                        product(bank(4 + b % 2), turned[:, b % 2, 0:P]).then_inc(s_mm, 1)

            def from_rows(w, width):
                return lambda ps, t: T.matmul(ps[:, 0:width], t, w, start=True, stop=True)

            pe.wait_ge(s_rows, 1)
            pe.wait_ge(s_node, 2)
            T.matmul(bank(0)[:, 0:NB], upto[:], deg[:], start=True, stop=True)
            T.matmul(bank(1)[:, 0:NB], ones[:], deg[:], start=True, stop=True).then_inc(s_rank, 1)
            pe.wait_ge(s_w, 16 * (1 + len(ONCE)))
            pe.wait_ge(s_rows, 2)
            pe.wait_ge(s_hs, 5)
            in_turn(pe, 3, sums(0, 3))
            pe.wait_ge(s_rows, 3)
            for i in range(NB + 2):
                if i < NB:
                    turn(i, agg, 0)
                if 1 <= i <= NB:
                    b = i - 1
                    pe.wait_ge(s_trc, b + 1)
                    if b >= 2:
                        pe.wait_ge(s_hidr, b - 1)
                    for k in range(HC):
                        mm = T.matmul(bank(2 + b % 2)[:, k * P:(k + 1) * P], weights["L0_W1T"][:, k * P:(k + 1) * P],
                                      turned[:, b % 2, 0:P], start=True, stop=True, skip_group_check=True)
                    mm.then_inc(s_hid, 1)
                if i >= 2:
                    b = i - 2
                    pe.wait_ge(s_hidr, b + 1)
                    if b >= 2:
                        pe.wait_ge(s_res, b - 1)
                    for k in range(HC):
                        mm = T.matmul(bank(4 + b % 2)[:, 0:D], hidden[:, b % 2, k, :], weights["L0_W2T"][:, k, :],
                                      start=(k == 0), stop=(k == HC - 1))
                    mm.then_inc(s_mm, 1)
            pe.wait_ge(s_hs, 10)
            in_turn(pe, 3, sums(1, 3))
            pe.wait_ge(s_hs, 15)
            in_turn(pe, 3, sums(2, 3))
            pe.wait_ge(s_rows, 7)
            turned_products(agg, NB, NB, lambda ps, t: T.matmul(ps[:, 0:P], weights["L1_W1"][:], t,
                                                                start=True, stop=True))
            for i in range(7):
                c = slice(i * 512, min(NP, (i + 1) * 512))
                pe.wait_ge(s_z, i + 1)
                if i >= 2:
                    pe.wait_ge(s_res, 2 * NB + i - 1)
                T.matmul(bank(4 + i % 2)[:, 0:c.stop - c.start], weights["L1_W2"][:], ft[:, c], start=True,
                         stop=True).then_inc(s_mm, 1)
            pe.wait_ge(s_rows, 11)
            turned_products(None, 2 * NB, 2 * NB + 7, lambda ps, t: T.transpose(ps[:, 0:P], t, identity[:]))
            pe.wait_ge(s_hs, 20)
            in_turn(pe, 3, sums(3, 3))
            pe.wait_ge(s_rows, 14)
            turned_products(agg, 3 * NB, 3 * NB + 7, from_rows(weights["L2_W1"][:], D))
            pe.wait_ge(s_hs, 25)
            in_turn(pe, 3, sums(4, 3))
            pe.wait_ge(s_rows, 16)
            turned_products(agg, 4 * NB, 4 * NB + 7, from_rows(weights["L2_W2"][:], D))
            with pe.Fori(0, LAYERS) as l:
                def told(k):
                    return V_LAYER * l + V_X3 + k

                pe.wait_ge(s_rows, V_X3)
                pe.wait_ge(s_lm, 16 * l + 16)
                pe.wait_ge(s_lw, 16 * len(LATER) * l + 16 * len(LATER))
                trcs, mms, ress = 3 * NB * l + 5 * NB, 3 * NB * l + MM3, 2 * NB * l + MM3
                lrows = weights["L3_rows"]
                for i in range(NB + 1):
                    if i < NB:
                        if i % GB == 0:
                            pe.wait_ge(s_grp, NG * l + (i // GB + 1))
                        turn(i, x, trcs)
                    if i >= 1:
                        b = i - 1
                        pe.wait_ge(s_trc, trcs + (b + 1))
                        if b >= 2:
                            pe.wait_ge(s_res, ress + (b - 1))
                            pe.wait_ge(s_ab, NB * l + (b - 1))
                        T.matmul(bank(4 + b % 2)[:, 0:D], turned[:, b % 2, 0:P], weights["M"][:, 0:D], start=True,
                                 stop=True)
                        T.matmul(bank(6 + b % 2)[:, 0:2 * D], turned[:, b % 2, 0:P], weights["M"][:, D:3 * D],
                                 start=True, stop=False)
                        T.matmul(bank(6 + b % 2)[:, 0:2 * D], ones[0:1, :],
                                 lrows[0:1, 0:2, :].rearrange("p a f -> p (a f)"), start=False,
                                 stop=True).then_inc(s_mm, 1)
                pe.wait_ge(s_hs, 10 * l + 35)
                pe.sem_inc(s_past, 1)
                flag = pe.value_load(overflow[0:1, 0:1], min_val=0, max_val=1)

                def chunks(b, slot, turn_):
                    at = [NB * q // QT for q in range(QT + 1)]
                    at[QT] = NB - 1
                    banks = [bank(4 + 2 * slot), bank(5 + 2 * slot)]
                    for q in range(QT):
                        c = NCH * l + QT * b + q
                        pe.wait_ge(s_gat[q], 64 * NB * l + 64 * b + 64)
                        pe.wait_ge(s_scan, c + 1)
                        for t in range(QT):
                            mm = T.transpose(bank(q % 2)[:, t * P:(t + 1) * P], rows_g[:, q, t, :], identity[:])
                        mm.then_inc(s_fwd, 1)
                        if q == 0:
                            pe.wait_ge(s_slab[slot], 16 * ([13, 12][slot] * l + (5 * SLABS[slot] + turn_)) + 16)
                            pe.wait_ge(s_agg, NB * l + (5 * NB + 2) + b)
                        if q < QT - 1:
                            for k in range(at[q], at[q + 1]):
                                for ps, part in zip(banks, (0, 3)):
                                    T.matmul(ps[:, 0:3 * D], slab[slot][:, k * P:(k + 1) * P],
                                             hs[:, k, part:part + 3, :].rearrange("p s f -> p (s f)"),
                                             start=(k == 0), stop=False, skip_group_check=True)
                        else:
                            count_products(pe, banks, (0, 3), slab[slot], range(at[q], NB - 1), flag, l + 5, b)
                        pe.wait_ge(s_scan, c + 3)
                        pe.wait_ge(s_rr, c + 1)
                        for t in range(QT):
                            for e in range(2):
                                mm = T.transpose(psum[:, 1024 + (2 * t + e) * P:1024 + (2 * t + e + 1) * P],
                                                 runs[q % 2][:, e, t * P:(t + 1) * P], identity[:])
                        mm.then_inc(s_back, 1)

                in_turn(pe, 2, chunks)
                pe.wait_ge(s_rows, told(3))
                pe.wait_ge(s_std, S_LAYER * l + (S_X3 + 1))
                for i in range(NB + 2):
                    if i < NB:
                        if i % GB == 0:
                            pe.wait_ge(s_merged, NG * l + (i // GB + 1))
                        if i >= 2:
                            pe.wait_ge(s_trc, trcs + (NB + i - 1))
                        for j, rows in enumerate((ends[:, i, 0, :], ends[:, i, 1, :], ft[:, i * P:(i + 1) * P],
                                                  agg[:, i, :])):
                            mm = T.transpose(bank(i % 2)[:, j * P:(j + 1) * P], rows, identity[:])
                        mm.then_inc(s_tr, 1)
                    if 1 <= i <= NB:
                        b = i - 1
                        pe.wait_ge(s_trc, trcs + (NB + b + 1))
                        if b >= 2:
                            pe.wait_ge(s_u, NB * l + (b - 1))
                        for j in range(4):
                            mm = T.matmul(bank(2 + b % 2)[:, 0:3 * D], turned[:, b % 2, j * P:(j + 1) * P],
                                          weights["U"][:, j, :], start=(j == 0), stop=(j == 3))
                        mm.then_inc(s_mm, 1)
                    if i >= 2:
                        b = i - 2
                        pe.wait_ge(s_u, NB * l + (b + 1))
                        if b >= 2:
                            pe.wait_ge(s_act, NB * l + (b - 1))
                        T.transpose(bank(4 + b % 2)[:, 0:P], u_row[:, b % 2, :], identity[:]).then_inc(s_ut, 1)
                pe.wait_ge(s_rows, told(5))
                turned_products(None, 3 * NB * l + 7 * NB, 2 * NB * l + (MM3 + NB), from_rows(weights["mix"][:], D))


_OUT = ((N, D), "float32")


def columns(*vectors):
    return np.stack(vectors, axis=1)


def on_all(*rows):
    return np.broadcast_to(np.stack(rows), (P, len(rows), D))


def lay_out(a):
    src = np.arange(TP * P, dtype=np.int32) % N
    dst = np.full((TP * P,), NP - 1, np.int32)
    src[:E], dst[:E] = a["src"], a["dst"]
    attr = np.zeros((AE, TP * P), np.float32)
    attr[:AE - 1, :E] = a["edge_attr_32"].T
    attr[AE - 1] = 1.0
    x = np.zeros((NP, D), np.float32)
    x[:N] = a["x"]
    mw, uw = a["L3_gnn_Mw"], a["L3_gnn_Uw"]
    u = [[uw[l, :, i * D:(i + 1) * D].T for i in range(13)] for l in range(LAYERS)]
    return {
        "in_x": x.reshape(NB, P, D).transpose(1, 0, 2),
        "in_src_col": src.reshape(TP, P).T,
        "in_dst_col": dst.reshape(TP, P).T,
        "in_dst_rows": dst[:NCH * CH].reshape(NCH, CH),
        "in_dst_prev": np.concatenate([np.full((1,), -1, np.int32), dst[:NCH * CH - 1]]).reshape(NCH, CH),
        "in_attrT": attr,
        "in_We": np.concatenate([a["L1_gnn_We"], a["L1_gnn_be"][None, :]]),
        "in_L0_W1T": a["L0_gnn_W1"].T,
        "in_L0_b1": a["L0_gnn_b1"].reshape(HC, P).T,
        "in_L0_W2T": a["L0_gnn_W2"].T.reshape(HC, P, D).transpose(1, 0, 2),
        "in_L1_W1": a["L1_gnn_W1"],
        "in_L1_W2": a["L1_gnn_W2"],
        "in_L1_cols": columns(*(a["L1_gnn_" + v] for v in ("b1", "g1", "beta1", "b2", "g2", "beta2")),
                              np.broadcast_to(a["L1_gnn_epsilon"], (P,))),
        "in_L2_W1": a["L2_gnn_W1"],
        "in_L2_W2": a["L2_gnn_W2"],
        "in_rows": on_all(a["L0_gnn_b2"], a["L2_gnn_b1"], a["L2_gnn_b2"]),
        "in_M": np.stack([np.concatenate([mw[l, :, :D].T, mw[l, :, D:].T, u[l][0]], axis=1) for l in range(LAYERS)]),
        "in_U": np.stack([np.stack([np.concatenate([u[l][1 + j], u[l][5 + j], u[l][9 + j]], axis=1)
                                    for j in range(4)], axis=1) for l in range(LAYERS)]),
        "in_mix": a["L3_gnn_mix_w"].transpose(0, 2, 1),
        "in_L3_rows": np.stack([on_all(a["L3_gnn_Mb"][l], a["L3_gnn_Ub"][l], a["L3_gnn_mix_b"][l],
                                       a["L3_gnn_ln_g"][l], a["L3_gnn_ln_b"][l]) for l in range(LAYERS)]),
        "in_L3_cols": np.stack([columns(a["L3_gnn_bn_g"][l], a["L3_gnn_bn_b"][l]) for l in range(LAYERS)]),
    }


def kernel(**inputs):
    import concourse.bacc as _bacc
    from concourse import mybir as _mybir
    from concourse.bass_utils import run_bass_kernel_spmd as _run

    arrays = {k: np.ascontiguousarray(v) for k, v in lay_out({k: np.asarray(v) for k, v in inputs.items()}).items()}
    nc = _bacc.Bacc("TRN2", target_bir_lowering=False, num_devices=1)
    ins = {k: nc.dram_tensor(k, v.shape, _mybir.dt.from_np(v.dtype), kind="ExternalInput").ap()
           for k, v in arrays.items()}
    out = nc.dram_tensor("out_dram", _OUT[0], F32, kind="ExternalOutput").ap()
    gnn_kernel(nc, ins, out)
    r = _run(nc, [arrays], core_ids=[0])
    return r.results[0]["out_dram"]
```

```python
from contextlib import ExitStack

import numpy as np

import concourse.bass as bass
from concourse import mybir

F32 = mybir.dt.float32
BF16 = mybir.dt.bfloat16
F16 = mybir.dt.float16
I32 = mybir.dt.int32
ALU = mybir.AluOpType
ACT = mybir.ActivationFunctionType
AX = mybir.AxisListType
RMAX = bass.bass_isa.ReduceOp.max
ds = bass.ds

P = 128
N = 3125
E = 50000
D = 128
NB = -(-N // P)
NP = NB * P
HID = 512
HC = HID // P
AE = 33
LAYERS = 3
GB = 5
NG = NB // GB
QT = 4
CH = QT * P
NCH = -(-E // CH)
LASTQ = NCH - QT * (NB - 1)
assert 0 < LASTQ <= QT and LASTQ % 2 == 0
TD = -(-E // P) + 1
TD += TD % 2
EQ = -(-E // CH)
TP = QT * QT * NB
MID = NP // 2
BIG = 4096.0
FAR = -3.0e38
MARK = 1.5e38
ROUND = 8388608.0
BN_EPS = 1e-5
CB = 512
NCB = -(-NP // CB)
ACC = NB * P
V_X3, V_LAYER = 18, 5
S_X3, S_LAYER = 6, 2
MM3 = 5 * NB + 7
DVE_LAYER = 81
SLABS_LAYER = [13, 12]
CALLS = 5
SLABS = [9, 8, 8]


WEIGHTS = {
    "L0_W1T": [P, HID], "L0_b1": [P, HC], "L0_W2T": [P, HC, D],
    "L1_W1": [P, D], "L1_W2": [P, D], "L1_cols": [P, 7],
    "L2_W1": [P, D], "L2_W2": [P, D],
    "rows": [P, 3, D],
    "M": [P, 3 * D], "U": [P, 4, 3 * D], "mix": [P, D],
    "L3_rows": [P, 5, D],
    "L3_cols": [P, 2],
}
LATER = ["U", "mix", "L3_rows", "L3_cols"]
ONCE = [w for w in WEIGHTS if w not in ("M", "U", "mix", "L3_rows", "L3_cols")]


def gnn_kernel(nc, ins, out):
    at_part = [nc.dram_tensor(f"at_part{i}", [NB, P, NB * P], BF16, kind="Internal").ap() for i in range(2)]
    a_dram = nc.dram_tensor("a_dram", [NP, D], F32, kind="Internal").ap()
    x3_dram = nc.dram_tensor("x3_dram", [P, NB, D], F32, kind="Internal").ap()
    scan_dram = nc.dram_tensor("scan_dram", [NCH * CH + 1, 2 * D], F32, kind="Internal").ap()
    mask_dram = nc.dram_tensor("mask_dram", [NCH, 2 * CH], BF16, kind="Internal").ap()

    with ExitStack() as ctx:
        def sb(name, shape, dt):
            return ctx.enter_context(nc.sbuf_tensor(name, shape, dt))

        def sem(name):
            return ctx.enter_context(nc.semaphore(name))

        psum = ctx.enter_context(nc.psum_tensor("psum", [P, 8 * 512], F32))

        identity = sb("identity", [P, P], F32)
        src_col = sb("src_col", [P, TP], I32)
        ranges = sb("ranges", [P, 64], I32)
        deg = sb("deg", [P, NB], F32)
        edge_sum = sb("edge_sum", [P, NB, D], F32)
        overflow = sb("overflow", [P, 1], I32)
        x = sb("x", [P, NB, D], F32)
        weights = {name: sb("w_" + name, shape, F32) for name, shape in WEIGHTS.items()}
        d_self = sb("d_self", [P, NB], F32)
        root = sb("root", [P, NB], F32)
        dinv = sb("dinv", [P, NB], F32)
        rdeg = sb("rdeg", [P, NB], F32)
        log4 = sb("log4", [P, NB], F32)
        inv4 = sb("inv4", [P, NB], F32)
        upto = sb("upto", [P, P], F32)
        ones = sb("ones", [P, P], F32)
        end_idx = sb("end_idx", [P, NB], I32)
        end_f = sb("end_f", [P, NB], F32)
        total_f = sb("total_f", [P, NB + 1], F32)
        some = sb("some", [P, NB], F32)
        far_row = sb("far_row", [1, 2 * D], F32)
        stats = sb("stats", [P, NB, 6], F32)
        mv = sb("mv", [P, NB, 2], F32)
        rstd = sb("rstd", [P, NB], F32)
        std = sb("std", [P, NB], F32)
        cstats = sb("cstats", [P, 7, 6], F32)
        cmv = sb("cmv", [P, 2], F32)
        cstd = sb("cstd", [P, 1], F32)
        cscale = sb("cscale", [P, 1], F32)
        cshift = sb("cshift", [P, 1], F32)
        eps = sb("eps", [P, 2], F32)
        one_eps = sb("one_eps", [P, 1], F32)

        bctx = ExitStack()

        def sbb(name, shape, dt):
            return bctx.enter_context(nc.sbuf_tensor(name, shape, dt))

        iota_src = sbb("iota_src", [P, NP], F16)
        iota_dst = sbb("iota_dst", [P, P], F32)
        block_base = sbb("block_base", [P, NB + 1], F32)
        zeros = sbb("zeros", [P, 512], BF16)
        ones_col = sbb("ones_col", [P, 1], F32)
        dst_col = sbb("dst_col", [P, TP], I32)
        src_off = sbb("src_off", [P, TP], F32)
        dst_f = sbb("dst_f", [P, TP], F32)
        onehot_src = sbb("onehot_src", [P, 2, NP], BF16)
        onehot_dst = sbb("onehot_dst", [P, 4, 2, P], BF16)
        deg_to = sbb("deg_to", [P, NB + 1], F32)
        onehot_sum = sbb("onehot_sum", [P, P], F32)
        attr_ring = sbb("attr_ring", [AE, 4, 2 * P], F32)
        attr_now = sbb("attr_now", [AE, 2 * P], F32)
        we = sbb("we", [AE, D], F32)
        ef32 = sbb("ef32", [P, 2, D], F32)
        ef_rest = sbb("ef_rest", [P, 2, D], F32)
        ef_split = sbb("ef_split", [P, 2, 2, 3 * D], BF16)
        a32 = sbb("a32", [P, NB * P], F32)
        a_part = [sbb(f"a_part{i}", [P, NB * P], BF16) for i in range(2)]
        a_most = sbb("a_most", [P, NB * P], BF16)
        most = sbb("most", [P, 2], F32)
        rows_i = sbb("rows_i", [P, CH], I32)
        prev_i = sbb("prev_i", [P, CH], I32)
        mask_rows = sbb("mask_rows", [P, 2, CH], BF16)
        rows_f = sbb("rows_f", [P, CH], F32)
        prev_f = sbb("prev_f", [P, CH], F32)
        t_min = sbb("t_min", [P, QT], F32)
        t_max = sbb("t_max", [P, QT], F32)
        t_next = sbb("t_next", [P, QT], F32)
        t_left = sbb("t_left", [P, QT], F32)
        b_lo = sbb("b_lo", [P, NB], F32)
        b_hi = sbb("b_hi", [P, NB], F32)
        touch = sbb("touch", [P, 2, NB], F32)
        reach = sbb("reach", [P, 2, NB], F32)
        reach_all = sbb("reach_all", [P, 2, NB], F32)
        rng_f = sbb("rng_f", [P, 64], F32)
        first = sbb("first", [P, NB + 1], F32)
        end = sbb("end", [P, NB + 1], F32)
        steps = sbb("steps", [P, NB], F32)

        bctx.close()

        hs = sb("hs", [P, NB, 6, D], BF16)
        slab = [sb(f"slab{i}", [P, NB * P], BF16) for i in range(3)]
        slab_rest = sb("slab_rest", [P, NB * P], BF16)
        agg = sb("agg", [P, NB, D], F32)
        g = sb("g", [P, NB, D], F32)
        ft = sb("ft", [P, NP], F32)
        ft2 = sb("ft2", [P, NP], F32)
        turned = sb("turned", [P, 2, 4 * D], F32)
        hidden = sb("hidden", [P, 2, HC, P], F32)
        idx_now = sb("idx_now", [P, QT, QT], I32)
        rows_g = sb("rows_g", [P, QT, QT, D], F32)
        marks = [sb(f"marks{i}", [P, 2 * CH], BF16) for i in range(2)]
        runs = [sb(f"runs{i}", [P, 2, CH], F32) for i in range(2)]
        run_rows = [sb(f"run_rows{i}", [P, QT, 2 * D], F32) for i in range(2)]
        var_tmp = sb("var_tmp", [P, 4, D], F32)
        var_now = sb("var_now", [P, D], F32)
        std_now = sb("std_now", [P, D], F32)
        vturned = sb("vturned", [P, 2 * D], F32)
        u_row = sb("u_row", [P, 2, D], F32)
        ends = hs[:].rearrange("p b s f -> p (b s f)").bitcast(F32)[:, 0:NB * 2 * D].rearrange(
            "p (b s f) -> p b s f", b=NB, s=2)

        s_lists = sem("s_lists")
        s_we = sem("s_we")
        s_const = sem("s_const")
        s_prime = sem("s_prime")
        s_dve = sem("s_dve")
        s_casts = sem("s_casts")
        s_reach = sem("s_reach")
        s_reached = sem("s_reached")
        s_ranges = sem("s_ranges")
        s_mask = sem("s_mask")
        s_mask_out = sem("s_mask_out")
        s_attr = sem("s_attr")
        s_attr_now = sem("s_attr_now")
        s_ef_mm = sem("s_ef_mm")
        s_ef32 = sem("s_ef32")
        s_ef_hi = sem("s_ef_hi")
        s_ef_r1 = sem("s_ef_r1")
        s_ef_mid = sem("s_ef_mid")
        s_ef_lo = sem("s_ef_lo")
        s_oh = sem("s_oh")
        s_oh_sum = sem("s_oh_sum")
        s_tile = sem("s_tile")
        s_block = sem("s_block")
        s_deg_mm = sem("s_deg_mm")
        s_ev_first = sem("s_ev_first")
        s_ev_act = sem("s_ev_act")
        s_ev_dve = sem("s_ev_dve")
        s_part0 = sem("s_part0")
        s_part1 = sem("s_part1")
        s_most = sem("s_most")
        s_store0 = sem("s_store0")
        s_store1 = sem("s_store1")
        s_flag = sem("s_flag")

        s_w = sem("s_w")
        s_far = sem("s_far")
        s_node = sem("s_node")
        s_act = sem("s_act")
        s_rank = sem("s_rank")
        s_hi = sem("s_hi")
        s_r1 = sem("s_r1")
        s_mid = sem("s_mid")
        s_hs = sem("s_hs")
        s_slab = [sem(f"s_slab{i}") for i in range(3)]
        s_slab_rest = sem("s_slab_rest")
        s_rest_used = sem("s_rest_used")
        s_spmm = sem("s_spmm")
        s_agg = sem("s_agg")
        s_tr = sem("s_tr")
        s_trc = sem("s_trc")
        s_mm = sem("s_mm")
        s_res = sem("s_res")
        s_hid = sem("s_hid")
        s_hidr = sem("s_hidr")
        s_rows = sem("s_rows")
        s_group = sem("s_group")
        s_std = sem("s_std")
        s_x3 = sem("s_x3")
        s_lm = sem("s_lm")
        s_lw = sem("s_lw")
        s_merged = sem("s_merged")
        s_y = sem("s_y")
        s_neg = sem("s_neg")
        s_e = sem("s_e")
        s_grp = sem("s_grp")
        s_bu = sem("s_bu")
        s_ab = sem("s_ab")
        s_a_out = sem("s_a_out")
        s_idx = sem("s_idx")
        s_gat = [sem(f"s_gat{i}") for i in range(QT)]
        s_mk = [sem(f"s_mk{i}") for i in range(2)]
        s_fwd = sem("s_fwd")
        s_scan = sem("s_scan")
        s_back = sem("s_back")
        s_rr = sem("s_rr")
        s_st = [sem(f"s_st{i}") for i in range(2)]
        s_fin = sem("s_fin")
        s_var = sem("s_var")
        s_var_now = sem("s_var_now")
        s_std_now = sem("s_std_now")
        s_vtr = sem("s_vtr")
        s_vturned = sem("s_vturned")
        s_vmm = sem("s_vmm")
        s_take = sem("s_take")
        s_vu = sem("s_vu")
        s_ends = [sem(f"s_ends{i}") for i in range(NG)]
        s_u = sem("s_u")
        s_ut = sem("s_ut")
        s_z = sem("s_z")
        s_out = sem("s_out")
        s_past = sem("s_past")

        lists = {"in_src_col": src_col, "in_dst_col": dst_col}
        N_CONST = 10
        block = ctx.enter_context(nc.Block())

        def bank(i):
            return psum[:, i * 512:(i + 1) * 512]

        def chunks_with(b):
            return LASTQ if isinstance(b, int) and b == NB - 1 else QT

        def turned_at(nq):
            return 2 if nq > 2 else 0

        def after_first(eng, b, slot, part):
            if isinstance(b, int) or slot:
                part(b - 1)
            else:
                with eng.If(b > 0):
                    part((b - 1).with_bounds(min_val=0, max_val=NB - 1))

        def in_turn(eng, n, body):
            with eng.Fori(0, NB // n) as i:
                for s in range(n):
                    body(n * i + s, s, i)
            for s in range(NB % n):
                body(NB // n * n + s, s, NB // n)

        def load_pairs(eng, b):
            lo = eng.value_load(ranges[0:1, ds(b, 1)], min_val=0, max_val=NB * TD)
            hi = eng.value_load(ranges[0:1, ds(b + 1, 1)], min_val=1, max_val=NB * TD)
            return lo, hi

        def load_offset(eng, b):
            return eng.value_load(ranges[0:1, ds(b + 32, 1)], min_val=0, max_val=2 * NB * TD)

        def tile_of(m, off, j):
            t = 2 * m + j - off
            return t.with_bounds(min_val=0, max_val=TP - 2)

        @block.sync
        def _(sp):
            sp.dma_start(x[:], ins["in_x"]).then_inc(s_w, 16)
            for name in ONCE:
                sp.dma_start(weights[name][:], ins["in_" + name]).then_inc(s_w, 16)

            def layer_weights(names, l, sem):
                for name in names:
                    v = ins["in_" + name][ds(l, 1)]
                    v = v.rearrange("l p a b -> (l p) a b") if len(v.shape) == 4 else v.rearrange("l p a -> (l p) a")
                    sp.dma_start(weights[name][:], v).then_inc(sem, 16)

            layer_weights(["M"], 0, s_lm)
            layer_weights(LATER, 0, s_lw)
            for name, tile in lists.items():
                sp.dma_start(tile[:], ins[name]).then_inc(s_lists, 16)
            sp.dma_start(rows_i[0:NCH, :], ins["in_dst_rows"]).then_inc(s_lists, 16)
            sp.dma_start(prev_i[0:NCH, :], ins["in_dst_prev"]).then_inc(s_lists, 16)
            sp.dma_start(we[:], ins["in_We"]).then_inc(s_we, 16)
            sp.wait_ge(s_mask, 1)
            sp.dma_start(mask_dram, mask_rows[0:NCH].rearrange("p s e -> p (s e)")).then_inc(s_mask_out, 16)
            sp.wait_ge(s_ranges, 1)
            sp.wait_ge(s_prime, 1)
            with sp.Fori(0, NB) as b:
                lo, hi = load_pairs(sp, b)
                off = load_offset(sp, b)
                with sp.Fori(lo, hi) as m:
                    sp.wait_ge(s_attr_now, m + 1)
                    sp.wait_ge(s_attr, 16 * m + 16)
                    sp.dma_start(attr_ring[:, ds(m % 4, 1), :],
                                 ins["in_attrT"][:, ds(tile_of(m, off, 0) * P, 2 * P)]).then_inc(s_attr, 16)
            total = sp.value_load(ranges[0:1, NB:NB + 1], min_val=1, max_val=NB * TD)
            for k in range(2):
                last = sp.snap(total + k)
                sp.wait_ge(s_prime, 1)
                sp.wait_ge(s_attr_now, last + 1)
                sp.wait_ge(s_attr, 16 * last + 16)
                sp.dma_start(attr_ring[:, ds(last % 4, 1), :], ins["in_attrT"][:, 0:2 * P]).then_inc(s_attr, 16)

            def counts(c, n):
                sp.wait_ge(s_spmm, NB * c + 3)
                sp.sem_inc(s_past, 1)
                flag = sp.value_load(overflow[0:1, 0:1], min_val=0, max_val=1)

                def load(b, slot, turn):
                    sp.wait_ge(s_prime, 1)
                    sp.wait_ge(s_spmm, NB * c + b + (4 - n))
                    sp.dma_start(slab[slot][:], at_part[0][ds(b, 1)].rearrange("a p n -> (a p) n")).then_inc(
                        s_slab[slot], 16)
                    with sp.If(flag > 0):
                        sp.wait_ge(s_prime, 1)
                        sp.wait_ge(s_rest_used, NB * c + b + 1)
                        sp.dma_start(slab_rest[:], at_part[1][ds(b, 1)].rearrange("a p n -> (a p) n")).then_inc(
                            s_slab_rest, 16)
                return load

            sp.wait_ge(s_flag, 2)
            sp.wait_ge(s_store0, 16 * NB + 16)
            sp.wait_ge(s_store1, 16 * NB)
            sp.wait_ge(s_mask_out, 16)
            for c in range(CALLS):
                in_turn(sp, 3, counts(c, 3))
            sp.wait_ge(s_rows, V_X3)
            sp.dma_start(x3_dram, x[:]).then_inc(s_x3, 16)
            sp.wait_ge(s_x3, 16)
            with sp.Fori(0, LAYERS) as l:
                sp.wait_ge(s_prime, 1)
                sp.wait_ge(s_rows, V_LAYER * l + V_X3 + 1)
                sp.dma_start(a_dram.rearrange("(b p) f -> p b f", p=P), g[:]).then_inc(s_a_out, 16)
                load = counts(l + CALLS, 2)

                def block_loads(b, slot, turn):
                    load(b, slot, turn)
                    for q in range(chunks_with(b)):
                        c = QT * b + q
                        sp.wait_ge(s_prime, 1)
                        sp.wait_ge(s_scan, NCH * l + c + 1)
                        sp.dma_start(marks[q % 2][:],
                                     mask_dram[ds(c, 1), :].rearrange("a e -> (a e)").partition_broadcast(P)
                                     ).then_inc(s_mk[q % 2], 16)
                in_turn(sp, 2, block_loads)
                sp.wait_ge(s_prime, 1)
                sp.wait_ge(s_bu, NB * l + NB)
                layer_weights(["M"], (l + 1) % LAYERS, s_lm)
                sp.wait_ge(s_prime, 1)
                sp.wait_ge(s_y, NG * l + NG)
                layer_weights(LATER, (l + 1) % LAYERS, s_lw)
            sp.wait_ge(s_grp, NG * LAYERS + NG)
            sp.dma_start(g[:], x3_dram).then_inc(s_x3, 16)
            sp.wait_ge(s_rows, V_X3 + V_LAYER * LAYERS + 2)
            sp.dma_start(out[0:(NB - 1) * P, :].rearrange("(b p) f -> p b f", p=P), x[:, 0:NB - 1, :]).then_inc(
                s_out, 16)
            sp.dma_start(out[(NB - 1) * P:N, :], x[0:N - (NB - 1) * P, NB - 1, :]).then_inc(s_out, 16)
            sp.wait_ge(s_lm, 16 * (LAYERS + 1))
            sp.wait_ge(s_lw, 16 * len(LATER) * (LAYERS + 1))
            sp.wait_ge(s_out, 32)

        @block.gpsimd
        def _(pool):
            pool.sem_inc(s_ef_mm, 1)
            pool.sem_inc(s_ef_lo, 1)
            pool.sem_inc(s_ef_r1, 1)
            pool.sem_inc(s_ef32, 1)
            pool.sem_inc(s_attr_now, 4)
            pool.sem_inc(s_part0, 1)
            pool.sem_inc(s_attr, 16)
            pool.sem_inc(s_tile, 4)
            pool.sem_inc(s_ev_act, 1)
            pool.sem_inc(s_ev_dve, 1)
            pool.sem_inc(s_part1, 1)
            pool.sem_inc(s_most, 1)
            pool.sem_inc(s_store0, 16)
            pool.sem_inc(s_oh_sum, 7)
            pool.sem_inc(s_rest_used, 1)
            pool.sem_inc(s_spmm, 3)
            pool.sem_inc(s_agg, 3)
            pool.sem_inc(s_scan, 2)
            pool.sem_inc(s_back, 2)
            pool.sem_inc(s_rr, 1)
            pool.sem_inc(s_ut, 2)
            pool.sem_inc(s_vtr, 1)
            pool.sem_inc(s_var, 4)
            pool.sem_inc(s_vturned, 1)
            pool.sem_inc(s_vmm, 1)
            pool.sem_inc(s_take, 3)
            pool.sem_inc(s_vu, 1)
            pool.sem_inc(s_grp, NG)
            pool.sem_inc(s_st[0], 16)
            pool.sem_inc(s_st[1], 16)
            pool.sem_inc(s_prime, 1)
            nc.gpsimd.memset(far_row[:, 0:D], FAR)
            nc.gpsimd.memset(far_row[:, D:2 * D], -FAR)
            nc.gpsimd.memset(eps[:, 0:1], BN_EPS)
            nc.gpsimd.memset(eps[:, 1:2], 1e-30)
            nc.gpsimd.memset(total_f[:], 0.0)
            nc.gpsimd.memset(ones[:], 1.0).then_inc(s_node, 1)
            pool.wait_ge(s_node, 1)
            nc.gpsimd.affine_select(out=upto[:], in_=ones[:], compare_op=ALU.is_ge, fill=0.0, base=0,
                                    pattern=[[1, P]], channel_multiplier=-1).then_inc(s_node, 1)
            nc.gpsimd.iota(iota_src[:], [[1, NP]], base=-MID, channel_multiplier=0,
                           allow_small_or_imprecise_dtypes=True).then_inc(s_const, 1)
            nc.gpsimd.iota(iota_dst[:], [[1, P]], base=0, channel_multiplier=0,
                           allow_small_or_imprecise_dtypes=True).then_inc(s_const, 1)
            nc.gpsimd.iota(block_base[:], [[P, NB + 1]], base=0, channel_multiplier=0,
                           allow_small_or_imprecise_dtypes=True).then_inc(s_const, 1)
            nc.gpsimd.iota(t_next[:], [[1, QT]], base=1, channel_multiplier=QT,
                           allow_small_or_imprecise_dtypes=True).then_inc(s_const, 1)
            nc.gpsimd.memset(zeros[:], 0.0).then_inc(s_const, 1)
            nc.gpsimd.memset(ones_col[:], 1.0).then_inc(s_const, 1)
            nc.gpsimd.memset(onehot_sum[:], 0.0).then_inc(s_const, 1)
            nc.gpsimd.memset(a_part[0][:], 0.0).then_inc(s_const, 1)
            nc.gpsimd.memset(identity[:], 0.0).then_inc(s_const, 1)
            pool.wait_ge(s_const, 9)
            nc.gpsimd.affine_select(out=identity[:], in_=identity[:], compare_op=ALU.not_equal, fill=1.0,
                                    base=0, pattern=[[-1, P]], channel_multiplier=1).then_inc(s_const, 1)
            pool.wait_ge(s_reach, 1)
            nc.gpsimd.partition_all_reduce(reach_all[:].rearrange("p a b -> p (a b)"),
                                           reach[:].rearrange("p a b -> p (a b)"), P, RMAX).then_inc(s_reached, 1)
            def add_rows(m):
                for j in range(2):
                    pool.wait_ge(s_const, N_CONST)
                    pool.wait_ge(s_oh, 2 * m + (j + 1))
                    pool.wait_ge(s_oh_sum, 2 * m + (7 + j))
                    nc.gpsimd.tensor_tensor(onehot_sum[:], onehot_sum[:],
                                            onehot_dst[:, ds(m % 4, 1), j, :].rearrange("p a n -> p (a n)"),
                                            ALU.add).then_inc(s_oh_sum, 1)

            def second_part(b):
                pool.wait_ge(s_const, N_CONST)
                pool.wait_ge(s_part0, b + 2)
                nc.gpsimd.tensor_tensor(a_part[1][:], a32[:], a_part[0][:], ALU.subtract).then_inc(s_part1, 1)
                pool.wait_ge(s_const, N_CONST)
                pool.wait_ge(s_part1, b + 2)
                nc.gpsimd.dma_start(at_part[1][ds(b, 1)].rearrange("a p n -> (a p) n"),
                                    a_part[1][:]).then_inc(s_store1, 16)

            pool.wait_ge(s_ranges, 1)
            add_rows(pool.snap(pool.value_load(ranges[0:1, 0:1], min_val=0, max_val=1)))
            with pool.Fori(0, NB) as b:
                lo, hi = load_pairs(pool, b)
                add_rows(lo + 1)
                with pool.If(b > 0):
                    second_part((b - 1).with_bounds(min_val=0, max_val=NB - 1))
                with pool.Fori(lo + 2, hi) as m:
                    add_rows(m)
                pool.wait_ge(s_const, N_CONST)
                pool.wait_ge(s_deg_mm, b + 1)
                add_rows(hi)
                with pool.If(b > 0):
                    pool.wait_ge(s_const, N_CONST)
                    pool.wait_ge(s_store1, 16 * b)
            last = pool.snap(pool.value_load(ranges[0:1, 0:1], min_val=0, max_val=1) + (NB - 1))
            second_part(last.with_bounds(min_val=0, max_val=NB - 1))
            pool.wait_ge(s_most, NB + 3)
            nc.gpsimd.partition_all_reduce(most[:, 1:2], most[:, 0:1], P, RMAX).then_inc(s_flag, 1)

            pool.wait_ge(s_flag, 2)
            nc.gpsimd.memset(runs[1][:], 0.0).then_inc(s_node, 1)
            with pool.Fori(0, LAYERS) as l:
                pool.wait_ge(s_a_out, 16 * l + 16)
                pool.sem_inc(s_past, 1)
                def chunk_rows(b):
                    for q in range(chunks_with(b)):
                        pool.wait_ge(s_idx, TP // QT * l + QT * b + q + 1)
                        pool.sem_inc(s_past, 1)
                        for t in range(QT):
                            nc.gpsimd.indirect_dma_start(
                                rows_g[:, q, t, :], None, a_dram,
                                bass.IndirectOffsetOnAxis(ap=idx_now[:, q, t:t + 1], axis=0),
                                bounds_check=NP - 1, oob_is_err=False).then_inc(s_gat[q], 16)

                with pool.Fori(0, NB - 1) as b:
                    chunk_rows(b)
                chunk_rows(NB - 1)
                pool.wait_ge(s_prime, 1)
                for i in range(2):
                    pool.wait_ge(s_st[i], 16 * (NCH // 2) * l + 16 * (NCH // 2) + 16)
                pool.wait_ge(s_spmm, NB * l + NB * 6 + 3)
                pool.sem_inc(s_past, 1)
                for b in range(NB):
                    nc.gpsimd.indirect_dma_start(
                        ends[:, b, :, :].rearrange("p s f -> p (s f)"), None, scan_dram,
                        bass.IndirectOffsetOnAxis(ap=end_idx[:, b:b + 1], axis=0),
                        bounds_check=NCH * CH, oob_is_err=False).then_inc(s_ends[b // GB], 16)

        @block.vector
        def _(dve):
            made = [0]

            def step(ins_):
                made[0] += 1
                ins_.then_inc(s_dve, 1)
                dve.wait_ge(s_dve, made[0])

            dve.wait_ge(s_lists, 64)
            dve.wait_ge(s_const, N_CONST)
            nc.vector.tensor_scalar(src_off[:], src_col[:], -float(MID), None, ALU.add)
            nc.vector.tensor_copy(dst_f[:], dst_col[:]).then_inc(s_casts, 1)
            nc.vector.tensor_copy(prev_f[0:NCH, :], prev_i[0:NCH, :])
            step(nc.vector.tensor_copy(rows_f[0:NCH, :], rows_i[0:NCH, :]))
            step(nc.vector.tensor_tensor(prev_f[0:NCH, :], rows_f[0:NCH, :], prev_f[0:NCH, :], ALU.is_equal))
            step(nc.vector.tensor_scalar(prev_f[0:NCH, :], prev_f[0:NCH, :], -1.0, 1.0, ALU.mult, ALU.add))
            nc.vector.tensor_scalar(mask_rows[0:NCH, 0, :], prev_f[0:NCH, :], -MARK, None, ALU.mult)
            nc.vector.tensor_scalar(mask_rows[0:NCH, 1, :], prev_f[0:NCH, :], 2 * MARK, -MARK, ALU.mult,
                                    ALU.add).then_inc(s_mask, 1)
            rows = rows_f[0:EQ, :].rearrange("q (j e) -> q j e", j=QT)
            nc.vector.tensor_reduce(t_min[0:EQ, :], rows, AX.X, ALU.min)
            nc.vector.tensor_reduce(t_max[0:EQ, :], rows, AX.X, ALU.max)
            nc.vector.tensor_scalar(t_left[:], t_next[:], -1.0, BIG + 1, ALU.mult, ALU.add)
            nc.vector.tensor_copy(b_lo[:], block_base[:, 0:NB])
            nc.vector.tensor_scalar(b_hi[:], block_base[:, 0:NB], float(P - 1), None, ALU.add)
            step(nc.vector.memset(reach[:], 0.0))
            for j in range(QT):
                c = slice(j, j + 1)
                step(nc.vector.tensor_scalar(touch[0:EQ, 0, :], b_hi[0:EQ, :], t_min[0:EQ, c], None, ALU.is_ge))
                step(nc.vector.scalar_tensor_tensor(touch[0:EQ, 1, :], b_lo[0:EQ, :], t_max[0:EQ, c],
                                                    touch[0:EQ, 0, :], ALU.is_le, ALU.mult))
                for k, t in enumerate((t_left, t_next)):
                    step(nc.vector.scalar_tensor_tensor(reach[0:EQ, k, :], touch[0:EQ, 1, :], t[0:EQ, c],
                                                        reach[0:EQ, k, :], ALU.mult, ALU.max))
            nc.vector.memset(rng_f[:], 0.0)
            nc.vector.memset(first[:], 0.0)
            step(nc.vector.memset(end[:], 0.0))
            dve.wait_ge(s_dve, made[0])
            nc.vector.memset(steps[:], 0.0).then_inc(s_reach, 1)
            dve.wait_ge(s_reached, 1)
            step(nc.vector.tensor_tensor_scan(end[:, 1:NB + 1], reach_all[:, 1, :], reach_all[:, 1, :], 0.0,
                                              ALU.max, ALU.max))
            step(nc.vector.tensor_scalar(first[:, 0:NB], reach_all[:, 0, :], -1.0, BIG, ALU.mult, ALU.add))
            step(nc.vector.tensor_tensor(first[:, 0:NB], first[:, 0:NB], end[:, 0:NB], ALU.min))
            step(nc.vector.tensor_tensor(steps[:], end[:, 1:NB + 1], first[:, 0:NB], ALU.subtract))
            step(nc.vector.tensor_scalar(steps[:], steps[:], 0.5, 0.25, ALU.mult, ALU.add))
            step(nc.vector.tensor_scalar(steps[:], steps[:], ROUND, None, ALU.add))
            step(nc.vector.tensor_scalar(steps[:], steps[:], -ROUND, 3.0, ALU.add, ALU.max))
            step(nc.vector.tensor_tensor_scan(rng_f[:, 1:NB + 1], steps[:], steps[:], 0.0, ALU.add, ALU.max))
            step(nc.vector.scalar_tensor_tensor(rng_f[:, 32:33 + NB], rng_f[:, 0:NB + 1], 2.0, first[:],
                                                ALU.mult, ALU.subtract))
            nc.vector.tensor_copy(ranges[:], rng_f[:]).then_inc(s_ranges, 1)
            nc.vector.memset(deg_to[:], 0.0)
            step(nc.vector.memset(a_most[:], 0.0))
            dve.wait_ge(s_ranges, 1)

            def one_hots(j, m, b, off):
                t = tile_of(m, off, j)
                parts = ef_split[:, ds(m % 2, 1), :, :].rearrange("p a j f -> p (a j) f")
                if j == 0:
                    dve.wait_ge(s_ef_lo, m + 1)
                    dve.wait_ge(s_ef_hi, m + 1)
                    nc.vector.tensor_tensor(ef_rest[:], ef32[:], parts[:, :, 0:D], ALU.subtract).then_inc(s_ef_r1, 1)
                dve.wait_ge(s_tile, 2 * m + (j + 3))
                dve.wait_ge(s_oh_sum, 2 * m + (j + 1))
                nc.vector.tensor_scalar(onehot_src[:, j, :], iota_src[:], src_off[:, ds(t, 1)], None, ALU.is_equal)
                nc.vector.tensor_scalar(onehot_dst[:, ds(m % 4, 1), j, :].rearrange("p a n -> p (a n)"),
                                        iota_dst[:], block_base[:, ds(b, 1)],
                                        dst_f[:, ds(t, 1)], ALU.add,
                                        ALU.is_equal).then_inc(s_oh, 1)
                if j == 0:
                    dve.wait_ge(s_ef_mid, m + 1)
                    nc.vector.tensor_tensor(parts[:, :, 2 * D:3 * D], ef_rest[:], parts[:, :, D:2 * D],
                                            ALU.subtract).then_inc(s_ef_lo, 1)

            def largest(b):
                dve.wait_ge(s_part0, b + 1)
                dve.wait_ge(s_most, b + 1)
                nc.vector.tensor_tensor(a_most[:], a_most[:], a_part[0][:], ALU.max).then_inc(s_most, 1)

            off0 = dve.value_load(ranges[0:1, 32:33], min_val=0, max_val=2 * NB * TD)
            zero = dve.snap(dve.value_load(ranges[0:1, 0:1], min_val=0, max_val=1))
            one_hots(0, zero, 0, off0)
            one_hots(1, zero, 0, off0)
            with dve.Fori(0, NB) as b:
                lo, hi = load_pairs(dve, b)
                off = load_offset(dve, b)
                with dve.Fori(lo + 1, hi) as m:
                    one_hots(0, m, b, off)
                    one_hots(1, m, b, off)
                off_next = load_offset(dve, b + 1)
                one_hots(0, hi, b + 1, off_next)
                dve.wait_ge(s_block, b + 1)
                dve.wait_ge(s_part1, b + 1)
                nc.vector.tensor_copy(a32[:, 2048:ACC], psum[:, 2048:ACC])
                nc.vector.tensor_reduce(edge_sum[:, ds(b, 1), :].rearrange("p a f -> p (a f)"),
                                        psum[:, ACC:ACC + 3 * D].rearrange("p (s f) -> p f s", s=3),
                                        AX.X, ALU.add)
                dve.wait_ge(s_deg_mm, b + 1)
                nc.vector.tensor_copy(deg_to[:, ds(b + 1, 1)], psum[:, 0:1]).then_inc(s_ev_dve, 1)
                one_hots(1, hi, b + 1, off_next)
                largest(b)
            largest(NB)
            dve.wait_ge(s_ev_dve, NB + 1)
            nc.vector.tensor_tensor(deg[:], deg_to[:, 1:NB + 1], deg_to[:, 0:NB], ALU.subtract)
            dve.wait_ge(s_most, NB + 2)
            nc.vector.tensor_reduce(most[:, 0:1], a_most[:], AX.X, ALU.max).then_inc(s_most, 1)
            dve.wait_ge(s_flag, 1)
            nc.vector.tensor_scalar(overflow[:], most[:, 1:2], 256.0, None, ALU.is_ge).then_inc(s_flag, 1)


            V = nc.vector

            def blk(tile, b):
                return tile[:, b, :] if len(tile.shape) == 3 else tile[:, b * P:(b + 1) * P]

            def flat(tile):
                return tile[:].rearrange("p b f -> p (b f)")

            groups_done = [0]

            def by_groups(op):
                for b in range(NB):
                    ins_ = op(b)
                    if b % GB == GB - 1:
                        ins_.then_inc(s_group, 1)
                groups_done[0] += NG
                dve.wait_ge(s_group, groups_done[0])
                dve.sem_inc(s_rows, 1)

            def split(n, source, at):
                for i in range(NG):
                    group = slice(GB * i, GB * i + GB)
                    dve.wait_ge(s_hi, NG * n + (i + 1))
                    V.tensor_tensor(agg[:, group, :], source[:, group, :], hs[:, group, at, :],
                                    ALU.subtract).then_inc(s_r1, 1)
                for i in range(NG):
                    group = slice(GB * i, GB * i + GB)
                    dve.wait_ge(s_mid, NG * n + (i + 1))
                    V.tensor_tensor(hs[:, group, at + 2, :], agg[:, group, :], hs[:, group, at + 1, :],
                                    ALU.subtract).then_inc(s_hs, 1)
                dve.wait_ge(s_hs, NG * n + NG)

            finished = [0]

            def row(tile, b):
                return tile[:, ds(b, 1), :].rearrange("p a f -> p (a f)")

            def gather_sums(c, *finish):
                def take(b, slot, turn):
                    dve.wait_ge(s_spmm, NB * c + b + 4)
                    V.tensor_reduce(row(agg, b), bank(slot)[:, 0:3 * D].rearrange("p (s f) -> p f s", s=3),
                                    AX.X, ALU.add).then_inc(s_agg, 1)
                    dve.wait_ge(s_agg, NB * c + b + 4)
                    for j, next_step in enumerate(finish):
                        if j:
                            dve.wait_ge(s_fin, len(finish) * b + (finished[0] + j))
                        next_step(b, row(agg, b)).then_inc(s_fin, 1)
                in_turn(dve, 3, take)
                finished[0] += len(finish) * NB
                dve.wait_ge(s_fin, finished[0])

            def plus(tile):
                return lambda b, rows: V.tensor_tensor(rows, rows, row(tile, b), ALU.add)

            def times(col):
                return lambda b, rows: V.tensor_scalar(rows, rows, col[:, ds(b, 1)], None, ALU.mult)

            def layer_norm(source, stds):
                if source is not None:
                    for b in range(NB):
                        last = V.bn_stats(stats[:, b, :], source[:, b, :])
                    step(last)
                for b in range(NB):
                    last = V.bn_aggr(mv[:, b, :], stats[:, b, :])
                last.then_inc(s_rows, 1)
                dve.wait_ge(s_std, stds)
                step(V.reciprocal(rstd[:], std[:]))

            def normalized(target, source):
                return lambda b: V.tensor_scalar(target[:, b, :], source[:, b, :], mv[:, b, 0:1], rstd[:, b:b + 1],
                                                 ALU.subtract, ALU.mult)

            def chunk_stats(source, i):
                return V.bn_stats(cstats[:, i, :], source[:, i * CB:min(N, (i + 1) * CB)])

            def batch_norm(gamma, beta, stds):
                V.bn_aggr(cmv[:], cstats[:].rearrange("p a b -> p (a b)")).then_inc(s_rows, 1)
                dve.wait_ge(s_std, stds)
                step(V.reciprocal(cscale[:], cstd[:]))
                step(V.tensor_tensor(cscale[:], cscale[:], gamma, ALU.mult))
                step(V.tensor_tensor(cshift[:], cmv[:, 0:1], cscale[:], ALU.mult))
                V.tensor_tensor(cshift[:], beta, cshift[:], ALU.subtract).then_inc(s_rows, 1)

            def results(base, n, take):
                for b in range(n):
                    dve.wait_ge(s_mm, base + (b + 1))
                    take(b, bank(4 + b % 2)).then_inc(s_res, 1)

            step(V.tensor_scalar(d_self[:], deg[:], 1.0, None, ALU.add))
            V.tensor_copy(some[:], deg[:]).then_inc(s_rows, 1)
            cols, rows3 = weights["L1_cols"], weights["rows"]
            dve.wait_ge(s_w, 16 * (1 + len(ONCE)))
            V.tensor_scalar(one_eps[:], cols[:, 6:7], 1.0, None, ALU.add)
            dve.wait_ge(s_node, 2)
            dve.wait_ge(s_rank, 1)
            V.tensor_copy(end_f[:], bank(0)[:, 0:NB])
            step(V.tensor_copy(std[:], bank(1)[:, 0:NB]))
            step(V.tensor_tensor_scan(total_f[:, 1:NB + 1], std[:], std[:], 0.0, ALU.add, ALU.max))
            step(V.tensor_tensor(end_f[:], end_f[:], total_f[:, 0:NB], ALU.add))
            step(V.tensor_scalar(end_f[:], end_f[:], float(NCH * CH), -float(NCH * CH + 1), ALU.min, ALU.add))
            step(V.tensor_scalar(some[:], deg[:], 0.5, None, ALU.is_ge))
            step(V.tensor_tensor(end_f[:], end_f[:], some[:], ALU.mult))
            step(V.tensor_scalar(end_idx[:], end_f[:], float(NCH * CH), None, ALU.add))
            dve.wait_ge(s_std, 1)
            step(V.tensor_scalar(log4[:], log4[:], 0.25, None, ALU.mult))
            V.reciprocal(inv4[:], log4[:])
            V.reciprocal(rdeg[:], d_self[:])
            step(V.reciprocal(dinv[:], root[:]))
            dve.wait_ge(s_store0, 16 * NB + 16)
            dve.wait_ge(s_store1, 16 * NB)
            dve.wait_ge(s_mask_out, 16)
            by_groups(lambda b: V.tensor_scalar(g[:, b, :], x[:, b, :], dinv[:, b:b + 1], None, ALU.mult))
            split(0, g, 0)
            gather_sums(0, plus(g), times(dinv))
            dve.sem_inc(s_rows, 1)
            results(0, NB, lambda b, ps: V.tensor_scalar(g[:, b, :], ps[:, 0:D], dinv[:, b:b + 1], None, ALU.mult))
            dve.wait_ge(s_res, NB)
            dve.sem_inc(s_rows, 1)
            split(1, g, 0)
            gather_sums(1, plus(g),
                        lambda b, rows: V.scalar_tensor_tensor(rows, rows, dinv[:, ds(b, 1)], rows3[:, 0, :],
                                                               ALU.mult, ALU.add),
                        lambda b, rows: V.scalar_tensor_tensor(rows, rows, 0.0, row(x, b), ALU.max, ALU.add),
                        lambda b, rows: V.bn_stats(row(stats, b), rows))
            layer_norm(None, 2)
            by_groups(normalized(x, agg))
            split(2, x, 0)
            gather_sums(2, plus(edge_sum),
                        lambda b, rows: V.scalar_tensor_tensor(rows, row(x, b), one_eps[:, 0:1], rows,
                                                               ALU.mult, ALU.add))
            dve.sem_inc(s_rows, 1)
            for i in range(NCB):
                for b in range(i * CB // P, min(NB, (i + 1) * CB // P)):
                    dve.wait_ge(s_mm, NB + (b + 1))
                    V.tensor_scalar(blk(ft, b), bank(4 + b % 2)[:, 0:D], cols[:, 0:1], None, ALU.add).then_inc(s_res, 1)
                dve.wait_ge(s_res, NB + (b + 1))
                last = chunk_stats(ft, i)
            step(last)
            batch_norm(cols[:, 1:2], cols[:, 2:3], 3)
            for i in range(NCB):
                c = slice(i * CB, min(NP, (i + 1) * CB))
                dve.wait_ge(s_mm, 2 * NB + i + 1)
                V.tensor_scalar(ft2[:, c], bank(4 + i % 2)[:, 0:c.stop - c.start], cols[:, 3:4], None,
                                ALU.add).then_inc(s_res, 1)
                dve.wait_ge(s_res, 2 * NB + i + 1)
                last = chunk_stats(ft2, i)
            step(last)
            batch_norm(cols[:, 4:5], cols[:, 5:6], 4)
            for b in range(NB):
                dve.wait_ge(s_mm, 2 * NB + NCB + b + 1)
                V.tensor_tensor(agg[:, b, :], bank(4 + b % 2)[:, 0:D], x[:, b, :], ALU.add).then_inc(s_res, 1)
                dve.wait_ge(s_res, 2 * NB + NCB + b + 1)
                last = V.bn_stats(stats[:, b, :], agg[:, b, :])
            step(last)
            layer_norm(None, 5)
            by_groups(normalized(x, agg))
            split(3, x, 0)
            gather_sums(3, plus(x), times(rdeg))
            dve.sem_inc(s_rows, 1)
            results(3 * NB + 7, NB, lambda b, ps: V.tensor_tensor(g[:, b, :], ps[:, 0:D], rows3[:, 1, :], ALU.add))
            dve.wait_ge(s_res, 4 * NB + 7)
            by_groups(lambda b: V.scalar_tensor_tensor(g[:, b, :], g[:, b, :], 0.01, g[:, b, :], ALU.mult,
                                                       ALU.max))
            split(4, g, 0)
            gather_sums(4, plus(g), times(rdeg))
            dve.sem_inc(s_rows, 1)
            for b in range(NB):
                dve.wait_ge(s_mm, 4 * NB + NCB + b + 1)
                V.tensor_tensor(agg[:, b, :], bank(4 + b % 2)[:, 0:D], rows3[:, 2, :], ALU.add).then_inc(s_res, 1)
                dve.wait_ge(s_res, 4 * NB + NCB + b + 1)
                step(V.tensor_tensor(agg[:, b, :], agg[:, b, :], x[:, b, :], ALU.add))
                last = V.bn_stats(stats[:, b, :], agg[:, b, :])
            step(last)
            layer_norm(None, 6)
            by_groups(normalized(x, agg))
            lrows, lcols = weights["L3_rows"], weights["L3_cols"]
            at_entry = made[0]
            with dve.Fori(0, LAYERS) as l:
                def step(ins_):
                    made[0] += 1
                    ins_.then_inc(s_dve, 1)
                    dve.wait_ge(s_dve, DVE_LAYER * l + made[0])
                    dve.sem_inc(s_past, 1)

                def told(k):
                    return V_LAYER * l + V_X3 + k

                for q in range(QT):
                    V.tensor_copy(idx_now[:, q, :], src_col[:, q * QT:q * QT + QT]).then_inc(s_idx, 1)
                for b in range(NB):
                    dve.wait_ge(s_mm, 3 * NB * l + MM3 + (b + 1))
                    V.tensor_copy(g[:, b, :], bank(4 + b % 2)[:, 0:D]).then_inc(s_res, 1)
                dve.wait_ge(s_res, 2 * NB * l + MM3 + NB)
                V.tensor_copy(cstats[:, 0, 0:1], dinv[:, 0:1]).then_inc(s_rows, 1)
                V.tensor_tensor(ft[:], flat(g), flat(g), ALU.mult).then_inc(s_rows, 1)
                dve.wait_ge(s_rows, told(2))
                split(2 * l + 5, g, 0)
                split(2 * l + 6, ft[:].rearrange("p (b f) -> p b f", b=NB), 3)
                dve.wait_ge(s_lw, 16 * len(LATER) * l + 16 * len(LATER))
                dve.wait_ge(s_ab, NB * l + NB)
                dve.sem_inc(s_past, 1)

                def variances(b):
                    n = NB * l + b
                    dve.wait_ge(s_agg, n + (NB * 5 + 4))
                    V.tensor_tensor(var_tmp[:, 0, :], var_tmp[:, 0, :], row(g, b), ALU.add)
                    V.tensor_tensor(var_tmp[:, 1, :], var_tmp[:, 1, :], ft[:, ds(b * D, D)], ALU.add).then_inc(s_var, 1)
                    dve.wait_ge(s_var, 4 * n + 5)
                    V.tensor_scalar(var_tmp[:, 0:2, :], var_tmp[:, 0:2, :], rdeg[:, ds(b, 1)], None,
                                    ALU.mult).then_inc(s_var, 1)
                    dve.wait_ge(s_var, 4 * n + 6)
                    V.tensor_tensor(var_tmp[:, 2, :], var_tmp[:, 0, :], var_tmp[:, 0, :], ALU.mult).then_inc(s_var, 1)
                    dve.wait_ge(s_var, 4 * n + 7)
                    V.tensor_tensor(var_tmp[:, 3, :], var_tmp[:, 1, :], var_tmp[:, 2, :], ALU.subtract).then_inc(
                        s_var, 1)
                    dve.wait_ge(s_var, 4 * n + 8)
                    dve.wait_ge(s_vtr, n + 1)
                    V.tensor_scalar(var_now[:], var_tmp[:, 3, :], 0.0, None, ALU.max).then_inc(s_var_now, 1)

                def take_part(b):
                    n = NB * l + b
                    u0 = ft2[:, ds(b * D, D)]
                    ps = bank(7)
                    dve.wait_ge(s_vmm, n + 2)
                    V.tensor_tensor(row(edge_sum, b), row(edge_sum, b), lrows[:, 0, :], ALU.add)
                    V.scalar_tensor_tensor(u0, ps[:, D:2 * D], log4[:, ds(b, 1)], u0, ALU.mult, ALU.add).then_inc(
                        s_take, 1)
                    dve.wait_ge(s_take, 3 * n + 4)
                    V.scalar_tensor_tensor(u0, ps[:, 2 * D:3 * D], inv4[:, ds(b, 1)], u0, ALU.mult,
                                           ALU.add).then_inc(s_take, 1)
                    dve.wait_ge(s_take, 3 * n + 5)
                    V.tensor_tensor(u0, ps[:, 0:D], u0, ALU.add).then_inc(s_take, 1)
                    dve.wait_ge(s_take, 3 * n + 6)
                    V.tensor_tensor(u0, u0, lrows[:, 1, :], ALU.add).then_inc(s_vu, 1)

                def chunks(b, slot, turn):
                    for q in range(chunks_with(b)):
                        c = NCH * l + QT * b + q
                        dve.wait_ge(s_mk[q % 2], 16 * (NCH // 2) * l + 32 * b + 16 * (q // 2 + 1))
                        dve.wait_ge(s_fwd, c + 1)
                        if chunks_with(b) == QT:
                            V.tensor_copy(idx_now[:, q, :],
                                          src_col[:, ds((QT * b + (q + QT)) * QT, QT)]).then_inc(s_idx, 1)
                        dve.wait_ge(s_back, c + 1)
                        dve.wait_ge(s_scan, c + 2)
                        dve.wait_ge(s_node, 3)
                        before = runs[(q + 1) % 2]
                        V.tensor_tensor_scan(runs[q % 2][:, 0, :], marks[q % 2][:, 0:CH], bank(q % 2),
                                             before[:, 0, CH - 1:CH], ALU.add, ALU.max)
                        V.tensor_tensor_scan(runs[q % 2][:, 1, :], marks[q % 2][:, CH:2 * CH], bank(q % 2),
                                             before[:, 1, CH - 1:CH], ALU.max, ALU.min).then_inc(s_scan, 1)
                        if q == 0:
                            after_first(dve, b, slot, variances)
                    dve.wait_ge(s_spmm, NB * l + b + (NB * 5 + 4))
                    for k in range(2):
                        last = V.tensor_reduce(var_tmp[:, k, :], bank(4 + k)[:, 0:3 * D].rearrange(
                            "p (s f) -> p f s", s=3), AX.X, ALU.add)
                    last.then_inc(s_agg, 1)
                    after_first(dve, b, slot, take_part)

                in_turn(dve, 2, chunks)
                variances(NB - 1)
                take_part(NB - 1)
                dve.wait_ge(s_vu, NB * l + (NB + 1))

                def merge(i, part):
                    at = slice(GB * i, GB * i + GB)
                    if part == 0:
                        dve.wait_ge(s_ends[i], 16 * GB * l + 16 * GB)
                        V.tensor_tensor(ends[:, at, 0, :], ends[:, at, 0, :], g[:, at, :], ALU.max)
                    elif part == 1:
                        step(V.tensor_tensor(ends[:, at, 1, :], ends[:, at, 1, :], g[:, at, :], ALU.min))
                    else:
                        ins_ = V.tensor_tensor(ends[:, at, part - 2, :], ends[:, at, part - 2, :],
                                               edge_sum[:, at, :], ALU.add)
                        if part == 3:
                            ins_.then_inc(s_merged, 1)

                for part in range(4):
                    merge(0, part)
                for b in range(NB):
                    if b % GB < 4 and b // GB + 1 < NG:
                        merge(b // GB + 1, b % GB)
                    ps = bank(2 + b % 2)
                    u = u_row[:, b % 2, :]
                    dve.wait_ge(s_mm, 3 * NB * l + (MM3 + NB + b + 1))
                    dve.wait_ge(s_ut, NB * l + (b + 1))
                    step(V.scalar_tensor_tensor(u, ps[:, D:2 * D], log4[:, b:b + 1], blk(ft2, b), ALU.mult, ALU.add))
                    step(V.scalar_tensor_tensor(u, ps[:, 2 * D:3 * D], inv4[:, b:b + 1], u, ALU.mult, ALU.add))
                    V.tensor_tensor(u, ps[:, 0:D], u, ALU.add).then_inc(s_u, 1)
                    if b >= 3 and (b - 3) % (CB // P) == CB // P - 1:
                        dve.wait_ge(s_act, NB * l + (b - 2))
                        last = chunk_stats(flat(edge_sum), (b - 3) // (CB // P))
                dve.wait_ge(s_act, NB * l + NB)
                for i in range((NB - 3) // (CB // P), NCB):
                    last = chunk_stats(flat(edge_sum), i)
                step(last)
                batch_norm(lcols[:, 0:1], lcols[:, 1:2], S_LAYER * l + (S_X3 + 1))
                for i in range(NG):
                    at = slice(GB * i, GB * i + GB)
                    dve.wait_ge(s_res, 2 * NB * l + (MM3 + NB + GB * i + GB))
                    step(V.scalar_tensor_tensor(agg[:, at, :], agg[:, at, :], 0.01, agg[:, at, :], ALU.mult, ALU.max))
                    step(V.tensor_tensor(agg[:, at, :], agg[:, at, :], x[:, at, :], ALU.add))
                    for b in range(GB * i, GB * i + GB):
                        last = V.bn_stats(stats[:, b, :], agg[:, b, :])
                step(last)
                for b in range(NB):
                    last = V.bn_aggr(mv[:, b, :], stats[:, b, :])
                last.then_inc(s_rows, 1)
                dve.wait_ge(s_std, S_LAYER * l + (S_X3 + 2))
                step(V.reciprocal(rstd[:], std[:]))
                for i in range(NG + 1):
                    if i < NG:
                        for b in range(GB * i, GB * i + GB):
                            last = V.scalar_tensor_tensor(agg[:, b, :], agg[:, b, :], mv[:, b, 0:1], lrows[:, 3, :],
                                                          ALU.subtract, ALU.mult)
                        step(last)
                        for b in range(GB * i, GB * i + GB):
                            last = V.scalar_tensor_tensor(agg[:, b, :], agg[:, b, :], rstd[:, b:b + 1],
                                                          lrows[:, 4, :], ALU.mult, ALU.add)
                        last.then_inc(s_y, 1)
                    if i >= 1:
                        at = slice(GB * i - GB, GB * i)
                        dve.wait_ge(s_e, NG * l + i)
                        step(V.tensor_scalar(agg[:, at, :], agg[:, at, :], 0.0, -1.0, ALU.max, ALU.add))
                        V.tensor_tensor(x[:, at, :], agg[:, at, :], g[:, at, :], ALU.add).then_inc(s_grp, 1)
                dve.wait_ge(s_grp, NG * l + 2 * NG)
            assert made[0] - at_entry == DVE_LAYER, made[0] - at_entry
            made[0] += (LAYERS - 1) * DVE_LAYER

            def step(ins_):
                made[0] += 1
                ins_.then_inc(s_dve, 1)
                dve.wait_ge(s_dve, made[0])
            dve.wait_ge(s_x3, 32)
            step(V.tensor_tensor(flat(agg), flat(g), flat(x), ALU.add))
            layer_norm(agg, S_X3 + S_LAYER * LAYERS + 1)
            by_groups(normalized(x, agg))

        @block.scalar
        def _(act):
            act.wait_ge(s_ranges, 1)

            def attributes(m):
                act.wait_ge(s_attr, 16 * m + 32)
                act.wait_ge(s_ef_mm, m + 1)
                act.wait_ge(s_prime, 1)
                nc.scalar.copy(attr_now[:], attr_ring[:, ds(m % 4, 1), :].rearrange(
                    "p a b -> p (a b)")).then_inc(s_attr_now, 1)

            def edge_features(m):
                attributes(m + 1)
                act.wait_ge(s_ef_mm, m + 2)
                act.wait_ge(s_ef_r1, m + 1)
                act.wait_ge(s_prime, 1)
                nc.scalar.activation(ef32[:], psum[:, 3584:3840].rearrange("p (j f) -> p j f", j=2),
                                     ACT.Relu).then_inc(s_ef32, 1)
                act.wait_ge(s_ef32, m + 2)
                act.wait_ge(s_tile, 2 * m + 2)
                act.wait_ge(s_prime, 1)
                nc.scalar.copy(ef_split[:, ds(m % 2, 1), :, 0:D].rearrange("p a j f -> p (a j) f"),
                               ef32[:]).then_inc(s_ef_hi, 1)
                act.wait_ge(s_ef_r1, m + 2)
                act.wait_ge(s_prime, 1)
                nc.scalar.copy(ef_split[:, ds(m % 2, 1), :, D:2 * D].rearrange("p a j f -> p (a j) f"),
                               ef_rest[:]).then_inc(s_ef_mid, 1)

            zero = act.snap(act.value_load(ranges[0:1, 0:1], min_val=0, max_val=1))
            attributes(zero)
            edge_features(zero)
            def first_part(b):
                act.wait_ge(s_ev_act, b + 2)
                act.wait_ge(s_ev_dve, b + 2)
                act.wait_ge(s_most, b + 2)
                act.wait_ge(s_store0, 16 * b + 16)
                act.wait_ge(s_prime, 1)
                nc.scalar.copy(a_part[0][:], a32[:]).then_inc(s_part0, 1)
                act.wait_ge(s_part0, b + 2)
                act.wait_ge(s_prime, 1)
                act.dma_start(at_part[0][ds(b, 1)].rearrange("a p n -> (a p) n"), a_part[0][:]).then_inc(s_store0, 16)

            with act.Fori(0, NB) as b:
                lo, hi = load_pairs(act, b)
                edge_features(lo + 1)
                with act.If(b > 0):
                    first_part((b - 1).with_bounds(min_val=0, max_val=NB - 1))
                with act.Fori(lo + 2, hi) as m:
                    edge_features(m)
                edge_features(hi)
                act.wait_ge(s_block, b + 1)
                act.wait_ge(s_part1, b + 1)
                act.wait_ge(s_prime, 1)
                nc.scalar.copy(a32[:, 0:512], psum[:, 0:512]).then_inc(s_ev_first, 1)
                nc.scalar.copy(a32[:, 512:2048], psum[:, 512:2048]).then_inc(s_ev_act, 1)
            last = act.snap(act.value_load(ranges[0:1, 0:1], min_val=0, max_val=1) + (NB - 1))
            first_part(last.with_bounds(min_val=0, max_val=NB - 1))

            A = nc.scalar

            def split(n, source, at, groups=None, between=None):
                for i in range(NG):
                    group = slice(GB * i, GB * i + GB)
                    if groups is not None:
                        act.wait_ge(s_group, groups + (i + 1))
                    A.copy(hs[:, group, at, :], source[:, group, :]).then_inc(s_hi, 1)
                    if between:
                        between()
                for i in range(NG):
                    group = slice(GB * i, GB * i + GB)
                    act.wait_ge(s_r1, NG * n + (i + 1))
                    A.copy(hs[:, group, at + 1, :], agg[:, group, :]).then_inc(s_mid, 1)
                    if between:
                        between()

            def turned_blocks(trs, trcs, mms, width):
                for b in range(NB):
                    act.wait_ge(s_tr, trs + (b + 1))
                    if b >= 2:
                        act.wait_ge(s_mm, mms + (b - 1))
                    A.copy(turned[:, b % 2, 0:width], bank(b % 2)[:, 0:width]).then_inc(s_trc, 1)

            def root_of(rows, target, source, e):
                act.wait_ge(s_rows, rows)
                A.activation(target, source, ACT.Sqrt, bias=eps[:, e:e + 1]).then_inc(s_std, 1)

            act.wait_ge(s_flag, 2)
            act.dma_start(scan_dram[NCH * CH:NCH * CH + 1, :], far_row[:]).then_inc(s_far, 16)
            act.wait_ge(s_rows, 1)
            A.activation(log4[:], d_self[:], ACT.Ln, bias=ones[:, 0:1])
            A.activation(root[:], d_self[:], ACT.Sqrt).then_inc(s_std, 1)
            split(0, g, 0, groups=0)
            cols = weights["L1_cols"]
            for i in range(NB + 1):
                if i < NB:
                    act.wait_ge(s_tr, i + 1)
                    if i >= 2:
                        act.wait_ge(s_hid, i - 1)
                    A.copy(turned[:, i % 2, 0:D], bank(i % 2)[:, 0:D]).then_inc(s_trc, 1)
                if i >= 1:
                    b = i - 1
                    act.wait_ge(s_hid, b + 1)
                    if b >= 2:
                        act.wait_ge(s_mm, b - 1)
                    for k in range(HC):
                        last = A.activation(hidden[:, b % 2, k, :], bank(2 + b % 2)[:, k * P:(k + 1) * P], ACT.Relu,
                                            bias=weights["L0_b1"][:, k:k + 1])
                    last.then_inc(s_hidr, 1)
            act.wait_ge(s_rows, 4)
            split(1, g, 0)
            root_of(5, std[:], mv[:, :, 1], 0)
            split(2, x, 0, groups=NG)
            turned_blocks(NB, NB, NB, D)
            root_of(8, cstd[:], cmv[:, 1:2], 0)
            act.wait_ge(s_rows, 9)
            for i in range(7):
                c = slice(i * 512, min(NP, (i + 1) * 512))
                A.activation(ft[:, c], ft[:, c], ACT.Relu, bias=cshift[:, 0:1], scale=cscale[:, 0:1]).then_inc(s_z, 1)
            root_of(10, cstd[:], cmv[:, 1:2], 0)
            act.wait_ge(s_rows, 11)
            for b in range(NB):
                if b >= 2:
                    act.wait_ge(s_mm, 2 * NB + 7 + b - 1)
                A.activation(turned[:, b % 2, 0:D], ft2[:, b * P:(b + 1) * P], ACT.Relu, bias=cshift[:, 0:1],
                             scale=cscale[:, 0:1]).then_inc(s_trc, 1)
            root_of(12, std[:], mv[:, :, 1], 0)
            split(3, x, 0, groups=2 * NG)
            turned_blocks(2 * NB, 3 * NB, 3 * NB + 7, D)
            split(4, g, 0, groups=3 * NG)
            turned_blocks(3 * NB, 4 * NB, 4 * NB + 7, D)
            root_of(17, std[:], mv[:, :, 1], 0)
            act.wait_ge(s_far, 16)
            with act.Fori(0, LAYERS) as l:
                def told(k):
                    return V_LAYER * l + V_X3 + k

                mms = 3 * NB * l + MM3
                for b in range(NB):
                    act.wait_ge(s_tr, 2 * NB * l + 4 * NB + (b + 1))
                    A.copy(ft2[:, b * P:(b + 1) * P], bank(b % 2)[:, 0:P]).then_inc(s_trc, 1)
                taken, turns = [0], [0]

                def take_bu():
                    turns[0] += 1
                    while taken[0] < NB and taken[0] * 4 * NG < turns[0] * NB:
                        b = taken[0]
                        act.wait_ge(s_bu, NB * l + (b + 1))
                        A.copy(edge_sum[:, b, :], bank(6 + b % 2)[:, 0:D])
                        A.copy(ft2[:, b * P:(b + 1) * P], bank(6 + b % 2)[:, D:2 * D]).then_inc(s_ab, 1)
                        taken[0] += 1

                act.wait_ge(s_rows, told(1))
                split(2 * l + 5, g, 0, between=take_bu)
                act.wait_ge(s_rows, told(2))
                split(2 * l + 6, ft[:].rearrange("p (b f) -> p b f", b=NB), 3, between=take_bu)
                assert taken[0] == NB

                def deviations(b):
                    n = NB * l + b
                    act.wait_ge(s_var_now, n + 1)
                    act.wait_ge(s_prime, 1)
                    A.activation(std_now[:], var_now[:], ACT.Sqrt, bias=eps[:, 1:2]).then_inc(s_std_now, 1)

                def var_turned(b):
                    n = NB * l + b
                    act.wait_ge(s_vtr, n + 2)
                    act.wait_ge(s_vmm, n + 1)
                    act.wait_ge(s_prime, 1)
                    A.copy(vturned[:], bank(6)[:, 0:2 * D]).then_inc(s_vturned, 1)

                def chunk_extremes(b, slot, turn):
                    nq = chunks_with(b)
                    for q in range(nq):
                        if q == turned_at(nq) // 2:
                            after_first(act, b, slot, deviations)
                        c = NCH * l + QT * b + q
                        act.wait_ge(s_back, c + 3)
                        act.wait_ge(s_st[q % 2], 16 * (NCH // 2) * l + 32 * b + 16 * (q // 2 + 1))
                        act.wait_ge(s_prime, 1)
                        A.copy(run_rows[q % 2][:].rearrange("p t f -> p (t f)"), psum[:, 1024:2048]).then_inc(s_rr, 1)
                        act.wait_ge(s_rr, c + 2)
                        act.wait_ge(s_prime, 1)
                        act.dma_start(scan_dram[ds((QT * b + q) * CH, CH), :].rearrange("(t p) f -> p t f", p=P),
                                      run_rows[q % 2][:]).then_inc(s_st[q % 2], 16)
                        if q == turned_at(nq):
                            after_first(act, b, slot, var_turned)

                in_turn(act, 2, chunk_extremes)
                deviations(NB - 1)
                var_turned(NB - 1)
                for i in range(NB + 2):
                    if i < NB:
                        act.wait_ge(s_tr, 2 * NB * l + (5 * NB + i + 1))
                        if i >= 2:
                            act.wait_ge(s_mm, mms + (NB + i - 1))
                        A.copy(turned[:, i % 2, 0:2 * D], bank(i % 2)[:, 0:2 * D]).then_inc(s_trc, 1)
                    if i >= 2:
                        b = i - 2
                        act.wait_ge(s_ut, NB * l + (b + 3))
                        A.mul(edge_sum[:, b, :], bank(4 + b % 2)[:, 0:D], float(np.sqrt(np.float32(1.0 / N)))).then_inc(
                            s_act, 1)
                root_of(told(3), cstd[:], cmv[:, 1:2], 0)
                act.wait_ge(s_rows, told(4))
                for i in range(NB + 1):
                    if i < NB:
                        if i >= 2:
                            act.wait_ge(s_mm, mms + (2 * NB + i - 1))
                        A.activation(turned[:, i % 2, 0:D], edge_sum[:, i, :], ACT.Identity, bias=cshift[:, 0:1],
                                     scale=cscale[:, 0:1]).then_inc(s_trc, 1)
                    if i >= 1:
                        b = i - 1
                        act.wait_ge(s_mm, mms + (2 * NB + b + 1))
                        A.copy(agg[:, b, :], bank(4 + b % 2)[:, 0:D]).then_inc(s_res, 1)
                root_of(told(5), std[:], mv[:, :, 1], 0)
                for i in range(NG):
                    at = slice(GB * i, GB * i + GB)
                    act.wait_ge(s_y, NG * l + (i + 1))
                    A.activation(g[:, at, :], agg[:, at, :], ACT.Relu, scale=-1.0).then_inc(s_neg, 1)
                    act.wait_ge(s_neg, NG * l + (i + 1))
                    A.activation(g[:, at, :], g[:, at, :], ACT.Exp, scale=-1.0).then_inc(s_e, 1)
            root_of(V_X3 + V_LAYER * LAYERS + 1, std[:], mv[:, :, 1], 0)

        @block.tensor
        def _(pe):
            def edge_features(m):
                pe.wait_ge(s_attr_now, m + 5)
                pe.wait_ge(s_ef32, m + 1)
                for j in range(2):
                    mm = nc.tensor.matmul(psum[:, 3584 + j * D:3584 + (j + 1) * D], attr_now[:, j * P:(j + 1) * P],
                                          we[:], start=True, stop=True)
                mm.then_inc(s_ef_mm, 1)

            pe.wait_ge(s_const, N_CONST)
            pe.wait_ge(s_we, 16)
            pe.wait_ge(s_ranges, 1)
            zero = pe.snap(pe.value_load(ranges[0:1, 0:1], min_val=0, max_val=1))
            edge_features(zero)
            edge_features(zero + 1)
            with pe.Fori(0, NB) as b:
                lo, hi = load_pairs(pe, b)
                pe.wait_ge(s_ev_act, b + 1)
                pe.wait_ge(s_ev_dve, b + 1)
                for k in range(7):
                    nc.tensor.matmul(psum[:, k * 512:k * 512 + 1], zeros[:, 0:P], zeros[:, 0:1], start=True,
                                     stop=False, skip_group_check=True)
                with pe.Fori(lo, hi) as m:
                    for j in range(2):
                        rows = onehot_dst[:, ds(m % 4, 1), j, :].rearrange("p a n -> p (a n)")
                        pe.wait_ge(s_oh, 2 * m + (j + 1))
                        for k in range(NB):
                            nc.tensor.matmul(psum[:, k * P:(k + 1) * P],
                                             onehot_src[:, j, k * P:(k + 1) * P], rows, start=False, stop=False,
                                             skip_group_check=True)
                        if j == 0:
                            pe.wait_ge(s_ef_lo, m + 2)
                        nc.tensor.matmul(psum[:, ACC:ACC + 3 * D], rows,
                                         ef_split[:, ds(m % 2, 1), j, :].rearrange("p a f -> p (a f)"),
                                         start=False, stop=False, skip_group_check=True).then_inc(s_tile, 1)
                        if j == 0:
                            edge_features(m + 2)
                for k in range(7):
                    mm = nc.tensor.matmul(psum[:, k * 512:k * 512 + 1], zeros[:, 0:P], zeros[:, 0:1], start=False,
                                          stop=True, skip_group_check=True)
                mm.then_inc(s_block, 1)
                pe.wait_ge(s_oh_sum, 2 * hi + 7)
                pe.wait_ge(s_ev_first, b + 1)
                nc.tensor.matmul(psum[:, 0:1], onehot_sum[:], ones_col[:], start=True, stop=True,
                                 skip_group_check=True).then_inc(s_deg_mm, 1)

            T = nc.tensor

            def sums(c, n):
                flag = pe.value_load(overflow[0:1, 0:1], min_val=0, max_val=1)

                def one(b, slot, turn):
                    pe.wait_ge(s_slab[slot], 16 * (SLABS[slot] * c + turn) + 16)
                    pe.wait_ge(s_agg, NB * c + b + 1)
                    count_products(pe, [bank(slot)], [0], slab[slot], range(NB - 1), flag, c, b)
                return one

            def count_products(pe, banks, ats, counts, ks, flag, c, b):
                for k in ks:
                    for ps, at in zip(banks, ats):
                        T.matmul(ps[:, 0:3 * D], counts[:, k * P:(k + 1) * P],
                                 hs[:, k, at:at + 3, :].rearrange("p s f -> p (s f)"), start=(k == 0), stop=False,
                                 skip_group_check=True)
                with pe.If(flag > 0):
                    pe.wait_ge(s_prime, 1)
                    pe.wait_ge(s_slab_rest, 16 * (NB * c + b) + 16)
                    for k in range(NB):
                        for ps, at in zip(banks, ats):
                            mm = T.matmul(ps[:, 0:3 * D], slab_rest[:, k * P:(k + 1) * P],
                                          hs[:, k, at:at + 3, :].rearrange("p s f -> p (s f)"), start=False,
                                          stop=False, skip_group_check=True)
                    mm.then_inc(s_rest_used, 1)
                k = NB - 1
                for ps, at in zip(banks, ats):
                    mm = T.matmul(ps[:, 0:3 * D], counts[:, k * P:(k + 1) * P],
                                  hs[:, k, at:at + 3, :].rearrange("p s f -> p (s f)"), start=False, stop=True,
                                  skip_group_check=True)
                mm.then_inc(s_spmm, 1)

            def turn(b, source, trcs):
                if b >= 2:
                    pe.wait_ge(s_trc, trcs + (b - 1))
                T.transpose(bank(b % 2)[:, 0:P], source[:, b, :], identity[:]).then_inc(s_tr, 1)

            def turned_products(source, trcs, ress, product):
                for i in range(NB + 1):
                    if i < NB and source is not None:
                        turn(i, source, trcs)
                    if i >= 1:
                        b = i - 1
                        pe.wait_ge(s_trc, trcs + (b + 1))
                        if b >= 2:
                            pe.wait_ge(s_res, ress + (b - 1))
                        product(bank(4 + b % 2), turned[:, b % 2, 0:P]).then_inc(s_mm, 1)

            def from_rows(w, width):
                return lambda ps, t: T.matmul(ps[:, 0:width], t, w, start=True, stop=True)

            pe.wait_ge(s_rows, 1)
            pe.wait_ge(s_node, 2)
            T.matmul(bank(0)[:, 0:NB], upto[:], deg[:], start=True, stop=True)
            T.matmul(bank(1)[:, 0:NB], ones[:], deg[:], start=True, stop=True).then_inc(s_rank, 1)
            pe.wait_ge(s_w, 16 * (1 + len(ONCE)))
            pe.wait_ge(s_rows, 2)
            pe.wait_ge(s_hs, 5)
            in_turn(pe, 3, sums(0, 3))
            pe.wait_ge(s_rows, 3)
            for i in range(NB + 2):
                if i < NB:
                    turn(i, agg, 0)
                if 1 <= i <= NB:
                    b = i - 1
                    pe.wait_ge(s_trc, b + 1)
                    if b >= 2:
                        pe.wait_ge(s_hidr, b - 1)
                    for k in range(HC):
                        mm = T.matmul(bank(2 + b % 2)[:, k * P:(k + 1) * P], weights["L0_W1T"][:, k * P:(k + 1) * P],
                                      turned[:, b % 2, 0:P], start=True, stop=True, skip_group_check=True)
                    mm.then_inc(s_hid, 1)
                if i >= 2:
                    b = i - 2
                    pe.wait_ge(s_hidr, b + 1)
                    if b >= 2:
                        pe.wait_ge(s_res, b - 1)
                    for k in range(HC):
                        mm = T.matmul(bank(4 + b % 2)[:, 0:D], hidden[:, b % 2, k, :], weights["L0_W2T"][:, k, :],
                                      start=(k == 0), stop=(k == HC - 1))
                    mm.then_inc(s_mm, 1)
            pe.wait_ge(s_hs, 10)
            in_turn(pe, 3, sums(1, 3))
            pe.wait_ge(s_hs, 15)
            in_turn(pe, 3, sums(2, 3))
            pe.wait_ge(s_rows, 7)
            turned_products(agg, NB, NB, lambda ps, t: T.matmul(ps[:, 0:P], weights["L1_W1"][:], t,
                                                                start=True, stop=True))
            for i in range(7):
                c = slice(i * 512, min(NP, (i + 1) * 512))
                pe.wait_ge(s_z, i + 1)
                if i >= 2:
                    pe.wait_ge(s_res, 2 * NB + i - 1)
                T.matmul(bank(4 + i % 2)[:, 0:c.stop - c.start], weights["L1_W2"][:], ft[:, c], start=True,
                         stop=True).then_inc(s_mm, 1)
            pe.wait_ge(s_rows, 11)
            turned_products(None, 2 * NB, 2 * NB + 7, lambda ps, t: T.transpose(ps[:, 0:P], t, identity[:]))
            pe.wait_ge(s_hs, 20)
            in_turn(pe, 3, sums(3, 3))
            pe.wait_ge(s_rows, 14)
            turned_products(agg, 3 * NB, 3 * NB + 7, from_rows(weights["L2_W1"][:], D))
            pe.wait_ge(s_hs, 25)
            in_turn(pe, 3, sums(4, 3))
            pe.wait_ge(s_rows, 16)
            turned_products(agg, 4 * NB, 4 * NB + 7, from_rows(weights["L2_W2"][:], D))
            with pe.Fori(0, LAYERS) as l:
                def told(k):
                    return V_LAYER * l + V_X3 + k

                pe.wait_ge(s_rows, V_X3)
                pe.wait_ge(s_lm, 16 * l + 16)
                trcs, mms, ress = 3 * NB * l + 5 * NB, 3 * NB * l + MM3, 2 * NB * l + MM3
                for i in range(NB + 1):
                    if i < NB:
                        if i % GB == 0:
                            pe.wait_ge(s_grp, NG * l + (i // GB + 1))
                        turn(i, x, trcs)
                    if i >= 1:
                        b = i - 1
                        pe.wait_ge(s_trc, trcs + (b + 1))
                        if b >= 2:
                            pe.wait_ge(s_res, ress + (b - 1))
                        T.matmul(bank(4 + b % 2)[:, 0:D], ft2[:, b * P:(b + 1) * P], weights["M"][:, 0:D],
                                 start=True, stop=True).then_inc(s_mm, 1)
                for b in range(NB):
                    if b >= 2:
                        pe.wait_ge(s_ab, NB * l + (b - 1))
                    T.matmul(bank(6 + b % 2)[:, 0:2 * D], ft2[:, b * P:(b + 1) * P], weights["M"][:, D:3 * D],
                             start=True, stop=True).then_inc(s_bu, 1)
                pe.wait_ge(s_lw, 16 * len(LATER) * l + 16 * len(LATER))
                pe.wait_ge(s_ab, NB * l + NB)
                pe.wait_ge(s_hs, 10 * l + 35)
                pe.sem_inc(s_past, 1)
                flag = pe.value_load(overflow[0:1, 0:1], min_val=0, max_val=1)

                def turn_var(b):
                    n = NB * l + b
                    pe.wait_ge(s_std_now, n + 1)
                    pe.wait_ge(s_vturned, n + 1)
                    T.transpose(bank(6)[:, 0:P], std_now[:], identity[:])
                    T.transpose(bank(6)[:, P:2 * P], var_now[:], identity[:]).then_inc(s_vtr, 1)

                def var_products(b):
                    n = NB * l + b
                    pe.wait_ge(s_vturned, n + 2)
                    pe.wait_ge(s_vu, n + 1)
                    T.matmul(bank(7)[:, 0:3 * D], vturned[:, 0:P], weights["U"][:, 2, :], start=True, stop=False)
                    T.matmul(bank(7)[:, 0:3 * D], vturned[:, P:2 * P], weights["U"][:, 3, :], start=False,
                             stop=True).then_inc(s_vmm, 1)

                def chunks(b, slot, turn_):
                    nq = chunks_with(b)
                    at = [NB * q // nq for q in range(nq)] + [NB - 1] if nq == QT else [0] + [NB - 1] * nq
                    banks = [bank(4), bank(5)]
                    for q in range(nq):
                        c = NCH * l + QT * b + q
                        pe.wait_ge(s_gat[q], 64 * (NB if q < LASTQ else NB - 1) * l + 64 * b + 64)
                        pe.wait_ge(s_scan, c + 1)
                        for t in range(QT):
                            mm = T.transpose(bank(q % 2)[:, t * P:(t + 1) * P], rows_g[:, q, t, :], identity[:])
                        mm.then_inc(s_fwd, 1)
                        if q == 0:
                            pe.wait_ge(s_slab[slot], 16 * (SLABS_LAYER[slot] * l + (CALLS * SLABS[slot] + turn_)) + 16)
                            pe.wait_ge(s_agg, NB * l + (5 * NB + 3) + b)
                        if q < nq - 1:
                            for k in range(at[q], at[q + 1]):
                                for ps, part in zip(banks, (0, 3)):
                                    T.matmul(ps[:, 0:3 * D], slab[slot][:, k * P:(k + 1) * P],
                                             hs[:, k, part:part + 3, :].rearrange("p s f -> p (s f)"),
                                             start=(k == 0), stop=False, skip_group_check=True)
                        else:
                            count_products(pe, banks, (0, 3), slab[slot], range(at[q], NB - 1), flag, l + 5, b)
                        if q == turned_at(nq):
                            after_first(pe, b, slot, turn_var)
                        if q == turned_at(nq) + 1:
                            after_first(pe, b, slot, var_products)
                        pe.wait_ge(s_scan, c + 3)
                        pe.wait_ge(s_rr, c + 1)
                        for t in range(QT):
                            for e in range(2):
                                mm = T.transpose(psum[:, 1024 + (2 * t + e) * P:1024 + (2 * t + e + 1) * P],
                                                 runs[q % 2][:, e, t * P:(t + 1) * P], identity[:])
                        mm.then_inc(s_back, 1)

                in_turn(pe, 2, chunks)
                turn_var(NB - 1)
                var_products(NB - 1)
                for i in range(NB + 2):
                    if i < NB:
                        if i % GB == 0:
                            pe.wait_ge(s_merged, NG * l + (i // GB + 1))
                        if i >= 2:
                            pe.wait_ge(s_trc, trcs + (NB + i - 1))
                        for j in range(2):
                            mm = T.transpose(bank(i % 2)[:, j * P:(j + 1) * P], ends[:, i, j, :], identity[:])
                        mm.then_inc(s_tr, 1)
                    if 1 <= i <= NB:
                        b = i - 1
                        pe.wait_ge(s_trc, trcs + (NB + b + 1))
                        if b >= 2:
                            pe.wait_ge(s_u, NB * l + (b - 1))
                        for j in range(2):
                            mm = T.matmul(bank(2 + b % 2)[:, 0:3 * D], turned[:, b % 2, j * P:(j + 1) * P],
                                          weights["U"][:, j, :], start=(j == 0), stop=(j == 1))
                        mm.then_inc(s_mm, 1)
                    if i >= 2:
                        b = i - 2
                        pe.wait_ge(s_u, NB * l + (b + 1))
                        if b >= 2:
                            pe.wait_ge(s_act, NB * l + (b - 1))
                        T.transpose(bank(4 + b % 2)[:, 0:P], u_row[:, b % 2, :], identity[:]).then_inc(s_ut, 1)
                pe.wait_ge(s_rows, told(4))
                
                def mixed(ps, t):
                    T.matmul(ps[:, 0:D], t, weights["mix"][:], start=True, stop=False)
                    return T.matmul(ps[:, 0:D], ones[0:1, :], weights["L3_rows"][0:1, 2, :], start=False, stop=True)

                turned_products(None, 3 * NB * l + 7 * NB, 2 * NB * l + (MM3 + NB), mixed)


_OUT = ((N, D), "float32")


def columns(*vectors):
    return np.stack(vectors, axis=1)


def on_all(*rows):
    return np.broadcast_to(np.stack(rows), (P, len(rows), D))


def lay_out(a):
    src = np.arange(TP * P, dtype=np.int32) % N
    dst = np.full((TP * P,), NP - 1, np.int32)
    src[:E], dst[:E] = a["src"], a["dst"]
    attr = np.zeros((AE, TP * P), np.float32)
    attr[:AE - 1, :E] = a["edge_attr_32"].T
    attr[AE - 1] = 1.0
    x = np.zeros((NP, D), np.float32)
    x[:N] = a["x"]
    mw, uw = a["L3_gnn_Mw"], a["L3_gnn_Uw"]
    u = [[uw[l, :, i * D:(i + 1) * D].T for i in range(13)] for l in range(LAYERS)]
    return {
        "in_x": x.reshape(NB, P, D).transpose(1, 0, 2),
        "in_src_col": src.reshape(TP, P).T,
        "in_dst_col": dst.reshape(TP, P).T,
        "in_dst_rows": dst[:NCH * CH].reshape(NCH, CH),
        "in_dst_prev": np.concatenate([np.full((1,), -1, np.int32), dst[:NCH * CH - 1]]).reshape(NCH, CH),
        "in_attrT": attr,
        "in_We": np.concatenate([a["L1_gnn_We"], a["L1_gnn_be"][None, :]]),
        "in_L0_W1T": a["L0_gnn_W1"].T,
        "in_L0_b1": a["L0_gnn_b1"].reshape(HC, P).T,
        "in_L0_W2T": a["L0_gnn_W2"].T.reshape(HC, P, D).transpose(1, 0, 2),
        "in_L1_W1": a["L1_gnn_W1"],
        "in_L1_W2": a["L1_gnn_W2"],
        "in_L1_cols": columns(*(a["L1_gnn_" + v] for v in ("b1", "g1", "beta1", "b2", "g2", "beta2")),
                              np.broadcast_to(a["L1_gnn_epsilon"], (P,))),
        "in_L2_W1": a["L2_gnn_W1"],
        "in_L2_W2": a["L2_gnn_W2"],
        "in_rows": on_all(a["L0_gnn_b2"], a["L2_gnn_b1"], a["L2_gnn_b2"]),
        "in_M": np.stack([np.concatenate([mw[l, :, :D].T, mw[l, :, D:].T, u[l][0]], axis=1) for l in range(LAYERS)]),
        "in_U": np.stack([np.stack([np.concatenate([u[l][1 + j], u[l][5 + j], u[l][9 + j]], axis=1)
                                    for j in range(4)], axis=1) for l in range(LAYERS)]),
        "in_mix": a["L3_gnn_mix_w"].transpose(0, 2, 1),
        "in_L3_rows": np.stack([on_all(a["L3_gnn_Mb"][l], a["L3_gnn_Ub"][l], a["L3_gnn_mix_b"][l],
                                       a["L3_gnn_ln_g"][l], a["L3_gnn_ln_b"][l]) for l in range(LAYERS)]),
        "in_L3_cols": np.stack([columns(a["L3_gnn_bn_g"][l], a["L3_gnn_bn_b"][l]) for l in range(LAYERS)]),
    }


def kernel(**inputs):
    import concourse.bacc as _bacc
    from concourse import mybir as _mybir
    from concourse.bass_utils import run_bass_kernel_spmd as _run

    arrays = {k: np.ascontiguousarray(v) for k, v in lay_out({k: np.asarray(v) for k, v in inputs.items()}).items()}
    nc = _bacc.Bacc("TRN2", target_bir_lowering=False, num_devices=1)
    ins = {k: nc.dram_tensor(k, v.shape, _mybir.dt.from_np(v.dtype), kind="ExternalInput").ap()
           for k, v in arrays.items()}
    out = nc.dram_tensor("out_dram", _OUT[0], F32, kind="ExternalOutput").ap()
    gnn_kernel(nc, ins, out)
    r = _run(nc, [arrays], core_ids=[0])
    return r.results[0]["out_dram"]
```
